# Optimizing a Trainium2 kernel written in Bass

```python
import numpy as np
import jax
import jax.numpy as jnp

def _softmax(x, axis=-1):
    return jax.nn.softmax(x, axis=axis)

def _gelu(x):
    return jax.nn.gelu(x, approximate=True)

def _silu(x):
    return jax.nn.silu(x)

def _sigmoid(x):
    return jax.nn.sigmoid(x)

def _layernorm(x, axis=-1, eps=1e-05):
    m = jnp.mean(x, axis=axis, keepdims=True)
    v = jnp.var(x, axis=axis, keepdims=True)
    return (x - m) / jnp.sqrt(v + eps)

def _scatter_add(tgt, idx, src, axis=0):
    return tgt.at[idx].add(src)

def _segment_sum(src, seg, n):
    return jax.ops.segment_sum(src, seg, n)
kernel_name = 'mk_decoder_preln_d1_seqx_r4_7a3bfb'

def setup_inputs(seed: int=0):
    np.random.seed(seed)
    _w = jnp.asarray

    def _rec_inputs():
        import jax
        import jax.numpy as jnp
        _rk = jax.random.key(seed)
        x = -0.0005207 + 1.001 * jax.random.normal(jax.random.fold_in(_rk, 1), (32, 100, 256), jnp.float32)
        _lenS = 100 - jax.random.randint(jax.random.fold_in(_rk, 7), (32,), 0, max(1, 100 // 4) + 1, jnp.int32)
        _lenS2 = 361 - jax.random.randint(jax.random.fold_in(_rk, 8), (32,), 0, max(1, 361 // 4) + 1, jnp.int32)
        _ctx_1024P = jax.random.normal(jax.random.fold_in(_rk, 11), (32, 16, 256), jnp.float32)
        _ctx_1024c = jax.random.dirichlet(jax.random.fold_in(_rk, 511), 0.3 * jnp.ones((16,), jnp.float32), (32, 361))
        _ctx_1024t = jnp.einsum('bsk,bkd->bsd', _ctx_1024c, _ctx_1024P)
        _ctx_1024t = _ctx_1024t * jax.lax.rsqrt(jnp.mean(jnp.square(_ctx_1024t)) + 1e-12) * 0.953939
        ctx_1024 = -0.000514642 + 1.00011 * (_ctx_1024t + 0.3 * jax.random.normal(jax.random.fold_in(_rk, 611), (32, 361, 256), jnp.float32))
        _validS = jnp.arange(100)[None, :] < _lenS[:, None]
        _validS2 = jnp.arange(361)[None, :] < _lenS2[:, None]
        _causal = jnp.tril(jnp.ones((100, 100), dtype=bool))
        mask_SxS2_ik0 = jnp.where(jnp.broadcast_to(_validS2[0:1, :], (100, 361)), 0, 1).astype(jnp.int32)
        return (x, ctx_1024, mask_SxS2_ik0)
    x, ctx_1024, mask_SxS2_ik0 = _rec_inputs()

    def _L0_attn_setup():
        import jax, jax.numpy as jnp
        import numpy as np
        D_MODEL = 256
        D_STATE = 128
        D_CONV = 4
        EXPAND = 2
        HEADDIM = 64
        D_INNER = EXPAND * D_MODEL
        NHEADS = D_INNER // HEADDIM
        CONV_DIM = D_INNER + 2 * D_STATE
        D_IN_PROJ = 2 * D_INNER + 2 * D_STATE + NHEADS
        BATCH, SEQLEN = (4, 512)
        EPS = 1e-05

        def _layernorm(u, w, b):
            mu = u.mean(-1, keepdims=True)
            var = ((u - mu) ** 2).mean(-1, keepdims=True)
            return (u - mu) * jax.lax.rsqrt(var + EPS) * w + b

        def _mamba2_block(x, ln_w, ln_b, in_proj_w, conv_w, conv_b, A_log, D, dt_bias, gamma, out_proj_w):
            Bsz, L, _ = x.shape
            u = _layernorm(x, ln_w, ln_b)
            zxbcdt = u @ in_proj_w.T
            z = zxbcdt[..., :D_INNER]
            xBC = zxbcdt[..., D_INNER:D_INNER + CONV_DIM]
            dt = jax.nn.softplus(zxbcdt[..., -NHEADS:] + dt_bias)
            xc = jnp.pad(xBC.transpose(0, 2, 1), ((0, 0), (0, 0), (D_CONV - 1, 0)))
            xc = jax.lax.conv_general_dilated(xc, conv_w[:, None, :], (1,), 'VALID', feature_group_count=CONV_DIM, dimension_numbers=('NCH', 'OIH', 'NCH'))
            xBC = jax.nn.silu(xc.transpose(0, 2, 1) + conv_b)
            xs = xBC[..., :D_INNER].reshape(Bsz, L, NHEADS, HEADDIM)
            Bm = xBC[..., D_INNER:D_INNER + D_STATE]
            Cm = xBC[..., D_INNER + D_STATE:]
            A = -jnp.exp(A_log)
            dA = jnp.exp(dt * A)

            def step(state, inp):
                dA_t, dt_t, x_t, B_t, C_t = inp
                state = state * dA_t[:, :, None, None] + (dt_t[:, :, None] * x_t)[..., None] * B_t[:, None, None, :]
                y = jnp.einsum('bhpn,bn->bhp', state, C_t)
                return (state, y)
            init = jnp.zeros((Bsz, NHEADS, HEADDIM, D_STATE), x.dtype)
            xs_scan = (dA.transpose(1, 0, 2), dt.transpose(1, 0, 2), xs.transpose(1, 0, 2, 3), Bm.transpose(1, 0, 2), Cm.transpose(1, 0, 2))
            _, ys = jax.lax.scan(step, init, xs_scan)
            y = ys.transpose(1, 0, 2, 3) + D[None, None, :, None] * xs
            y = y.reshape(Bsz, L, D_INNER)
            y = y * jax.nn.silu(z)
            y = y * jax.lax.rsqrt(jnp.mean(y * y, -1, keepdims=True) + EPS) * gamma
            return x + y @ out_proj_w.T
        key = jax.random.key(seed)
        ks = jax.random.split(key, 8)
        x = jax.random.normal(ks[0], (BATCH, SEQLEN, D_MODEL), jnp.float32)
        ln_w = jnp.ones((D_MODEL,), jnp.float32)
        ln_b = jnp.zeros((D_MODEL,), jnp.float32)
        in_proj_w = jax.random.normal(ks[1], (D_IN_PROJ, D_MODEL), jnp.float32) * 0.02
        conv_w = jax.random.normal(ks[2], (CONV_DIM, D_CONV), jnp.float32) * 0.1
        conv_b = jnp.zeros((CONV_DIM,), jnp.float32)
        A_log = jnp.log(jax.random.uniform(ks[3], (NHEADS,), jnp.float32, 1.0, 16.0))
        D = jnp.ones((NHEADS,), jnp.float32)
        dt = jax.random.uniform(ks[4], (NHEADS,), jnp.float32, 0.001, 0.1)
        dt_bias = dt + jnp.log(-jnp.expm1(-dt))
        gamma = jnp.ones((D_INNER,), jnp.float32)
        out_proj_w = jax.random.normal(ks[5], (D_MODEL, D_INNER), jnp.float32) * 0.02
        return dict(x=x, ln_w=ln_w, ln_b=ln_b, in_proj_w=in_proj_w, conv_w=conv_w, conv_b=conv_b, A_log=A_log, D=D, dt_bias=dt_bias, gamma=gamma, out_proj_w=out_proj_w)
    _L0_attn_all = _L0_attn_setup()
    _L0_attn_in = {k: v for k, v in _L0_attn_all.items() if k in ('ln_w', 'ln_b', 'in_proj_w', 'conv_w', 'conv_b', 'A_log', 'D', 'dt_bias', 'gamma', 'out_proj_w')}
    del _L0_attn_all

    def _L0_xattn_setup():
        import jax, jax.numpy as jnp
        import numpy as np
        import math
        B, S, D, H = (1, 512, 256, 16)
        DK = D // H
        key = jax.random.key(seed)
        ks = jax.random.split(key, 8)
        scale = 1.0 / math.sqrt(D)
        queries = jax.random.normal(ks[0], (B, S, D), dtype=jnp.float32)
        keys_ = jax.random.normal(ks[1], (B, S, D), dtype=jnp.float32)
        values = jax.random.normal(ks[2], (B, S, D), dtype=jnp.float32)
        mask = jnp.tril(jnp.ones((S, S), dtype=jnp.int32))
        Wq = jax.random.normal(ks[3], (H, D, DK), dtype=jnp.float32) * scale
        Wk = jax.random.normal(ks[4], (H, D, DK), dtype=jnp.float32) * scale
        Wv = jax.random.normal(ks[5], (H, D, DK), dtype=jnp.float32) * scale
        Wo = jax.random.normal(ks[6], (D, D), dtype=jnp.float32) * scale
        return {'queries': queries, 'keys': keys_, 'values': values, 'mask': mask, 'Wq': Wq, 'Wk': Wk, 'Wv': Wv, 'Wo': Wo}
    _L0_xattn_all = _L0_xattn_setup()
    _L0_xattn_in = {k: v for k, v in _L0_xattn_all.items() if k in ('Wq', 'Wk', 'Wv', 'Wo')}
    del _L0_xattn_all

    def _L0_ffn_setup():
        import jax, jax.numpy as jnp
        import numpy as np
        B, T, C = (2, 512, 256)
        E, H, TOPK = (8, 512, 2)
        key = jax.random.key(seed)
        k0, k1, k2, k3 = jax.random.split(key, 4)
        scale = 0.02
        return {'x': jax.random.normal(k0, (B, T, C), dtype=jnp.float32), 'Wg': jax.random.normal(k1, (C, E), dtype=jnp.float32) * scale, 'W1': jax.random.normal(k2, (E, C, H), dtype=jnp.float32) * scale, 'W2': jax.random.normal(k3, (E, H, C), dtype=jnp.float32) * scale}
    _L0_ffn_all = _L0_ffn_setup()
    _L0_ffn_in = {k: v for k, v in _L0_ffn_all.items() if k in ('Wg', 'W1', 'W2')}
    del _L0_ffn_all
    return {'x': x, 'ctx_1024': ctx_1024, 'mask_SxS2_ik0': mask_SxS2_ik0, 'L0_attn_ln_w': _L0_attn_in['ln_w'], 'L0_attn_ln_b': _L0_attn_in['ln_b'], 'L0_attn_in_proj_w': _L0_attn_in['in_proj_w'], 'L0_attn_conv_w': _L0_attn_in['conv_w'], 'L0_attn_conv_b': _L0_attn_in['conv_b'], 'L0_attn_A_log': _L0_attn_in['A_log'], 'L0_attn_D': _L0_attn_in['D'], 'L0_attn_dt_bias': _L0_attn_in['dt_bias'], 'L0_attn_gamma': _L0_attn_in['gamma'], 'L0_attn_out_proj_w': _L0_attn_in['out_proj_w'], 'L0_xattn_Wq': _L0_xattn_in['Wq'], 'L0_xattn_Wk': _L0_xattn_in['Wk'], 'L0_xattn_Wv': _L0_xattn_in['Wv'], 'L0_xattn_Wo': _L0_xattn_in['Wo'], 'L0_ffn_Wg': _L0_ffn_in['Wg'], 'L0_ffn_W1': _L0_ffn_in['W1'], 'L0_ffn_W2': _L0_ffn_in['W2']}

def reference(x, ctx_1024, mask_SxS2_ik0, L0_attn_ln_w, L0_attn_ln_b, L0_attn_in_proj_w, L0_attn_conv_w, L0_attn_conv_b, L0_attn_A_log, L0_attn_D, L0_attn_dt_bias, L0_attn_gamma, L0_attn_out_proj_w, L0_xattn_Wq, L0_xattn_Wk, L0_xattn_Wv, L0_xattn_Wo, L0_ffn_Wg, L0_ffn_W1, L0_ffn_W2):
    import jax
    import jax.numpy as jnp

    def _L0_attn_ref(x, ln_w, ln_b, in_proj_w, conv_w, conv_b, A_log, D, dt_bias, gamma, out_proj_w):
        import jax, jax.numpy as jnp
        import numpy as np
        D_MODEL = 256
        D_STATE = 128
        D_CONV = 4
        EXPAND = 2
        HEADDIM = 64
        D_INNER = EXPAND * D_MODEL
        NHEADS = D_INNER // HEADDIM
        CONV_DIM = D_INNER + 2 * D_STATE
        D_IN_PROJ = 2 * D_INNER + 2 * D_STATE + NHEADS
        BATCH, SEQLEN = (4, 512)
        EPS = 1e-05

        def _layernorm(u, w, b):
            mu = u.mean(-1, keepdims=True)
            var = ((u - mu) ** 2).mean(-1, keepdims=True)
            return (u - mu) * jax.lax.rsqrt(var + EPS) * w + b

        def _mamba2_block(x, ln_w, ln_b, in_proj_w, conv_w, conv_b, A_log, D, dt_bias, gamma, out_proj_w):
            Bsz, L, _ = x.shape
            u = _layernorm(x, ln_w, ln_b)
            zxbcdt = u @ in_proj_w.T
            z = zxbcdt[..., :D_INNER]
            xBC = zxbcdt[..., D_INNER:D_INNER + CONV_DIM]
            dt = jax.nn.softplus(zxbcdt[..., -NHEADS:] + dt_bias)
            xc = jnp.pad(xBC.transpose(0, 2, 1), ((0, 0), (0, 0), (D_CONV - 1, 0)))
            xc = jax.lax.conv_general_dilated(xc, conv_w[:, None, :], (1,), 'VALID', feature_group_count=CONV_DIM, dimension_numbers=('NCH', 'OIH', 'NCH'))
            xBC = jax.nn.silu(xc.transpose(0, 2, 1) + conv_b)
            xs = xBC[..., :D_INNER].reshape(Bsz, L, NHEADS, HEADDIM)
            Bm = xBC[..., D_INNER:D_INNER + D_STATE]
            Cm = xBC[..., D_INNER + D_STATE:]
            A = -jnp.exp(A_log)
            dA = jnp.exp(dt * A)

            def step(state, inp):
                dA_t, dt_t, x_t, B_t, C_t = inp
                state = state * dA_t[:, :, None, None] + (dt_t[:, :, None] * x_t)[..., None] * B_t[:, None, None, :]
                y = jnp.einsum('bhpn,bn->bhp', state, C_t)
                return (state, y)
            init = jnp.zeros((Bsz, NHEADS, HEADDIM, D_STATE), x.dtype)
            xs_scan = (dA.transpose(1, 0, 2), dt.transpose(1, 0, 2), xs.transpose(1, 0, 2, 3), Bm.transpose(1, 0, 2), Cm.transpose(1, 0, 2))
            _, ys = jax.lax.scan(step, init, xs_scan)
            y = ys.transpose(1, 0, 2, 3) + D[None, None, :, None] * xs
            y = y.reshape(Bsz, L, D_INNER)
            y = y * jax.nn.silu(z)
            y = y * jax.lax.rsqrt(jnp.mean(y * y, -1, keepdims=True) + EPS) * gamma
            return x + y @ out_proj_w.T
        return _mamba2_block(x, ln_w, ln_b, in_proj_w, conv_w, conv_b, A_log, D, dt_bias, gamma, out_proj_w)

    def _L0_xattn_ref(queries, keys, values, mask, Wq, Wk, Wv, Wo):
        import jax, jax.numpy as jnp
        import numpy as np
        import math
        B, S, D, H = (1, 512, 256, 16)
        DK = D // H
        q = jnp.einsum('bsd,hdk->bhsk', queries, Wq)
        k = jnp.einsum('bsd,hdk->bhsk', keys, Wk)
        v = jnp.einsum('bsd,hdk->bhsk', values, Wv)
        attn = jnp.einsum('bhsk,bhtk->bhst', q, k) / jnp.sqrt(jnp.asarray(DK, q.dtype))
        attn = jnp.where(mask == 0, -jnp.inf, attn)
        p = jax.nn.softmax(attn, axis=-1)
        o = jnp.einsum('bhst,bhtk->bhsk', p, v)
        o = o.transpose(0, 2, 1, 3).reshape(queries.shape[0], queries.shape[1], -1)
        out = jnp.einsum('bsd,ed->bse', o, Wo)
        return out

    def _L0_ffn_ref(x, Wg, W1, W2):
        import jax, jax.numpy as jnp
        import numpy as np
        B, T, C = (2, 512, 256)
        E, H, TOPK = (8, 512, 2)
        b, t, c = x.shape
        xf = x.reshape(-1, c)
        n = xf.shape[0]
        scores = xf @ Wg
        topk_scores, topk_idx = jax.lax.top_k(scores, TOPK)
        topk_probs = jax.nn.softmax(topk_scores, axis=-1)
        combine = jnp.zeros((n, E), dtype=xf.dtype)
        combine = combine.at[jnp.arange(n)[:, None], topk_idx].set(topk_probs)
        h = jnp.einsum('nc,ech->enh', xf, W1)
        h = jax.nn.silu(h)
        eo = jnp.einsum('enh,ehc->enc', h, W2)
        y = jnp.einsum('ne,enc->nc', combine, eo)
        return y.reshape(b, t, c)
    x = x + _L0_attn_ref(_layernorm(x, axis=-1), L0_attn_ln_w, L0_attn_ln_b, L0_attn_in_proj_w, L0_attn_conv_w, L0_attn_conv_b, L0_attn_A_log, L0_attn_D, L0_attn_dt_bias, L0_attn_gamma, L0_attn_out_proj_w)
    x = x + _L0_xattn_ref(_layernorm(x, axis=-1), ctx_1024, ctx_1024, mask_SxS2_ik0, L0_xattn_Wq, L0_xattn_Wk, L0_xattn_Wv, L0_xattn_Wo)
    x = x + _L0_ffn_ref(_layernorm(x, axis=-1), L0_ffn_Wg, L0_ffn_W1, L0_ffn_W2)
    return x

_drawn_inputs = setup_inputs


def setup_inputs(seed=0):
    import zlib

    import numpy as np

    out = dict(_drawn_inputs(seed))
    spreads = {'L0_attn_ln_w': (1.0, 0.2),
     'L0_attn_ln_b': (0.0, 0.315),
     'L0_attn_conv_b': (0.0, 0.1),
     'L0_attn_D': (1.0, 0.6),
     'L0_attn_gamma': (1.0, 0.2)}
    factors = {'L0_attn_A_log': 8.0, 'L0_attn_dt_bias': 8.0}
    for name, (base, spread) in spreads.items():
        noise = np.random.default_rng([zlib.crc32(name.encode()), seed]).standard_normal(out[name].shape)
        drawn = base * np.exp(spread * noise) if base else spread * noise
        out[name] = jnp.asarray(drawn.astype(out[name].dtype))
    for name, factor in factors.items():
        out[name] = (out[name] * factor).astype(out[name].dtype)
    return out
```

```python
from contextlib import ExitStack

import numpy as np
import concourse.bass as bass
from concourse import mybir

F32 = mybir.dt.float32
F32R = mybir.dt.float32r
I32 = mybir.dt.int32
ACT = mybir.ActivationFunctionType
ALU = mybir.AluOpType
AX = mybir.AxisListType

P = 128
SEQS, L, D = 32, 100, 256
KD = D // P
EPS = 1e-5

INNER, STATE, HEADS, HEADDIM, TAPS = 512, 128, 8, 64, 4
CONV = INNER + 2 * STATE
KX, KC = INNER // P, CONV // P
GROUP = 4
GROUPS = SEQS // GROUP
GL = GROUP * L
PRODUCT = [("dt", 0), ("conv", KX), ("gate", 0), ("conv", KX + 1), ("conv", 0), ("gate", 1), ("conv", 1),
           ("conv", 2), ("gate", 2), ("conv", 3), ("gate", 3)]
PRODUCTS = len(PRODUCT)
PARTS = [[0, 1, 2], [3, 4, 5], [6, 7, 8], [9, 10]]
LOG_TERMS = 6


def nth(kind, k):
    return sum(other == kind for other, _ in PRODUCT[:k])


def wait_before(eng, cell, waits):
    for s, v in waits:
        eng.wait_ge(s, v)
    eng.memset(cell, 0.0)


def bc_last(ap, n):
    return ap.unsqueeze(2).to_broadcast([ap.shape[0], ap.shape[1], n])


def bc_mid(ap, n):
    return ap.unsqueeze(1).to_broadcast([ap.shape[0], n, ap.shape[1]])


def mamba_block(nc, x_res, t):
    with ExitStack() as ctx:
        def sb(name, shape, dt=F32):
            return ctx.enter_context(nc.sbuf_tensor(name, shape, dt))

        def sem(name):
            return ctx.enter_context(nc.semaphore(name))

        w_in = sb("w_in", [P, KD, 2 * INNER + 2 * STATE + HEADS])
        w_out = sb("w_out", [P, KX, D])
        ln_w = sb("ln_w", [P, KD])
        ln_b = sb("ln_b", [P, KD])
        conv_w = sb("conv_w", [P, KC, TAPS])
        conv_b = sb("conv_b", [P, KC])
        gamma = sb("gamma", [P, KX])
        d_skip = sb("d_skip", [P, KX])
        a_neg = sb("a_neg", [L, HEADS])
        dt_bias = sb("dt_bias", [L, HEADS])
        ident = sb("ident_m", [P, P])
        upto = sb("upto", [L, L])
        after = sb("after", [L, L])
        ones = sb("ones_m", [P, 1])
        neg_half = sb("neg_half", [L, 2 * GROUP])

        stats = sb("stats", [L, GROUP, 6])
        mean_var = sb("mean_var", [L, GROUP, 2])
        var_eps = sb("var_eps", [L, 2, GROUP])
        rstd = sb("rstd", [L, 2, GROUP])
        res_scale = sb("res_scale", [L, GROUP])
        res_shift = sb("res_shift", [L, GROUP])
        normed = sb("normed", [L, GROUP, D])
        u_t = sb("u_t", [P, KD, GL])
        acc = sb("acc", [P, 2, GL])
        tanh = sb("tanh", [P, 2, GL])
        tanh_z = sb("tanh_z", [P, 2, GL])
        xbc = [sb(f"xbc{i}", [P, KC, GL]) for i in range(2)]
        gate = [sb(f"gate{i}", [P, KX, GL]) for i in range(2)]
        skip = [sb(f"skip{i}", [P, KX, GL]) for i in range(2)]
        dt_raw = sb("dt_raw", [L, GROUP, HEADS])
        dt_e = sb("dt_e", [L, GROUP, HEADS])
        dt_z = sb("dt_z", [L, GROUP, HEADS])
        dt_z2 = sb("dt_z2", [L, GROUP, HEADS])
        dt_p = sb("dt_p", [L, GROUP, HEADS])
        dt_8 = [sb(f"dt_8{i}", [L, GROUP, HEADS]) for i in range(2)]
        dt_a = [sb(f"dt_a{i}", [L, GROUP, HEADS]) for i in range(2)]

        steps = [sb(f"steps{i}", [L, HEADS, L]) for i in range(2)]
        decay = [sb(f"decay{i}", [L, HEADS, L]) for i in range(2)]
        cb = [sb(f"cb{i}", [L, L]) for i in range(2)]
        mix = [sb(f"mix{i}", [L, HEADS, L]) for i in range(2)]
        x_dt = [sb(f"x_dt{i}", [L, HEADS, HEADDIM]) for i in range(2)]
        y_skip = [sb(f"y_skip{i}", [P, KX, L]) for i in range(2)]
        gated = [sb(f"gated{i}", [P, KX, L]) for i in range(2)]
        squares = sb("squares", [P, KX, L])
        sq_half = sb("sq_half", [P, KX // 2, L])
        sq_sum = sb("sq_sum", [P, L])
        idle = sb("idle_m", [L, 1])
        ms = sb("ms", [L, 1])
        rms = sb("rms", [L, 1])

        psum = ctx.enter_context(nc.psum_tensor("psum_m", [P, 8, 512], F32))
        PROJ, CB, DECAY, XT, Y, OUT = 0, 2, 3, 5, 6, 7

        w_loaded = sem("w_loaded")
        x_loaded = sem("x_loaded")
        prep = sem("prep")
        a_ready = sem("a_ready")
        a_done = sem("a_done")
        v_stats = sem("v_stats")
        v_aggr = sem("v_aggr")
        v_var = sem("v_var")
        p_rstd = sem("p_rstd")
        v_res = sem("v_res")
        v_norm = sem("v_norm")
        pe_norm_t = sem("pe_norm_t")
        act_u = sem("act_u")
        pe_proj = sem("pe_proj")
        proj_used = sem("proj_used")
        act_tap = sem("act_tap")
        v_tap = sem("v_tap")
        act_tanh = sem("act_tanh")
        v_xbc = sem("v_xbc")
        act_zt = sem("act_zt")
        v_chain = sem("v_chain")
        act_dt = sem("act_dt")
        v_dt = sem("v_dt")
        p_skip = sem("p_skip")
        p_steps = sem("p_steps")
        pe_decay = sem("pe_decay")
        act_decay = sem("act_decay")
        pe_cb = sem("pe_cb")
        v_cb = sem("v_cb")
        pe_xt = sem("pe_xt")
        v_xdt = sem("v_xdt")
        p_mix = sem("p_mix")
        pe_y = sem("pe_y")
        v_yskip = sem("v_yskip")
        v_gated = sem("v_gated")
        act_sq = sem("act_sq")
        p_half = sem("p_half")
        p_sum = sem("p_sum")
        pe_out = sem("pe_out")
        v_ms = sem("v_ms")
        p_rms = sem("p_rms")
        v_x1 = sem("v_x1")

        WEIGHTS = 15
        x_view = t["x"].rearrange("s l d -> l s d")
        PREP = 2 + KX + 1
        CHAIN = 7 + LOG_TERMS

        def proj(k):
            return psum[:, PROJ + k % 2, 0:GL]

        def by_seq(ap):
            return ap.rearrange("p (b l) -> p b l", b=GROUP)

        def with_part(a_part, *hooks):
            if a_part:
                a_part(*hooks)
            else:
                for hook in hooks:
                    hook()

        def call_hooks(hooks, part, k):
            if hooks and k == PARTS[part][1]:
                hooks[0]()
            if hooks and k == PARTS[part][-1]:
                hooks[1]()

        def pipeline(eng, head, stage_a, stage_b, tail):
            head(0)
            for part in range(GROUP):
                stage_a(0, 0, part)
            def pair(g0, last):
                for i in range(2):
                    for q in range(GROUP):
                        more = not (last and i == 1)
                        stage_b(g0 + i, i, q, (lambda *hooks: stage_a(g0 + i + 1, 1 - i, q, hooks)) if more else None, not more and q == GROUP - 1)
            pair(0, False)
            with eng.Fori(1, GROUPS // 2 - 1) as m:
                pair(2 * m, False)
            pair(GROUPS - 2, True)
            tail()

        block = ctx.enter_context(nc.Block())

        @block.sync
        def _(sp):
            sp.dma_start(x_res[:, 0:GROUP, :], x_view[:, 0:GROUP, :]).then_inc(x_loaded, 16)
            loads = [
                (w_in[:], t["w_in"].rearrange("(k p) n -> p k n", p=P)),
                (w_out[:], t["w_out"].rearrange("(k p) n -> p k n", p=P)),
                (ln_w[:], t["ln_w"]), (ln_b[:], t["ln_b"]),
                (conv_w[:], t["conv_w"].rearrange("(i p) k -> p i k", p=P)),
                (conv_b[:], t["conv_b"]), (gamma[:], t["gamma"]),
                (a_neg[:], t["a_log"].partition_broadcast(L)),
                (dt_bias[:], t["dt_bias"].partition_broadcast(L)),
                (ident[:], t["ident"]), (upto[:], t["upto"]), (after[:], t["after"]),
            ]
            for dst, src in loads:
                sp.dma_start(dst, src).then_inc(w_loaded, 16)
            sp.dma_start(d_skip[0:HEADDIM, :], t["d_even"].partition_broadcast(HEADDIM)).then_inc(w_loaded, 16)
            sp.dma_start(d_skip[HEADDIM:P, :], t["d_odd"].partition_broadcast(HEADDIM)).then_inc(w_loaded, 16)
            sp.dma_start(ones[:], t["ones"]).then_inc(w_loaded, 16)
            for g in range(1, GROUPS):
                sp.wait_ge(x_loaded, 16 * g)
                sp.dma_start(x_res[:, g * GROUP:(g + 1) * GROUP, :],
                             x_view[:, g * GROUP:(g + 1) * GROUP, :]).then_inc(x_loaded, 16)

        @block.tensor
        def _(pe):
            pe.wait_ge(w_loaded, 16 * WEIGHTS)
            pe.wait_ge(prep, PREP)

            def head_half(g, k):
                if not (type(g) is int and g == 0):
                    pe.wait_ge(proj_used, g * PRODUCTS - 1 + k)
                pe.wait_ge(v_norm, g + 1)
                for b in range(GROUP):
                    last = pe.transpose(psum[:, PROJ + 1 - k, b * L:(b + 1) * L],
                                        normed[:, b, k * P:(k + 1) * P], ident[0:L, 0:L])
                last.then_inc(pe_norm_t, 1)

            def stage_a_head(g):
                for k in range(KD):
                    head_half(g, k)

            def stage_a(g, i, part, hooks=()):
                if part == 0:
                    pe.wait_ge(act_u, g + 1)
                for k in PARTS[part]:
                    kind, tile = PRODUCT[k]
                    call_hooks(hooks, part, k)
                    if k >= 2:
                        pe.wait_ge(proj_used, g * PRODUCTS + k - 1)
                    if kind == "dt":
                        for b in range(GROUP):
                            for d in range(KD):
                                last = pe.matmul(psum[0:L, PROJ + k % 2, b * HEADS:(b + 1) * HEADS],
                                                 u_t[:, d, b * L:(b + 1) * L], w_in[:, d, 2 * INNER + 2 * STATE:],
                                                 start=d == 0, stop=d == KD - 1)
                    else:
                        cols = (tile if kind == "gate" else KX + tile) * P
                        for d in range(KD):
                            last = pe.matmul(proj(k), w_in[:, d, cols:cols + P], u_t[:, d, :],
                                             start=d == 0, stop=d == KD - 1)
                    last.then_inc(pe_proj, 1)

            def out(n, j):
                pe.wait_ge(p_sum, n + 1)
                if not (type(n) is int and n == 0):
                    pe.wait_ge(v_x1, n)
                pe.matmul(psum[0:L, OUT, D:D + 1], sq_sum[:], ones[:], start=True, stop=True)
                for c in range(KX):
                    last = pe.matmul(psum[0:L, OUT, 0:D], gated[j][:, c, :], w_out[:, c, :],
                                     start=c == 0, stop=c == KX - 1)
                last.then_inc(pe_out, 1)

            def mix_tokens(n, j):
                pe.wait_ge(p_mix, n + 1)
                pe.wait_ge(v_xdt, n + 1)
                if not (type(n) is int and n == 0):
                    pe.wait_ge(v_yskip, n)
                for h in range(HEADS):
                    half = HEADDIM * (h % 2)
                    last = pe.matmul(psum[half:half + HEADDIM, Y, (h // 2) * L:(h // 2 + 1) * L],
                                     x_dt[j][:, h, :], mix[j][:, h, :], start=True, stop=True)
                last.then_inc(pe_y, 1)

            def stage_b(g, i, q, a_part, final):
                n, j = g * GROUP + q, q % 2
                first = type(n) is int and n == 0
                seq = slice(q * L, (q + 1) * L)
                head = q == 0 and a_part
                pe.wait_ge(p_steps, n + 1)
                if not first:
                    pe.wait_ge(act_decay, n)
                for half in range(2):
                    last = pe.matmul(psum[0:L, DECAY + half, 0:GL], after[:],
                                     steps[j][:, half * 4:half * 4 + 4, :], start=True, stop=True)
                last.then_inc(pe_decay, 1)
                if head:
                    head_half(g + 1, 0)
                pe.wait_ge(v_xbc, g * KC + 2)
                if not first:
                    pe.wait_ge(v_cb, n)
                pe.matmul(psum[0:L, CB, 0:L], xbc[i][:, KX, seq], xbc[i][:, KX + 1, seq],
                          start=True, stop=True).then_inc(pe_cb, 1)
                pe.wait_ge(v_xbc, (g + 1) * KC)
                if not first:
                    pe.wait_ge(v_xdt, n)
                for c in range(KX):
                    last = pe.transpose(psum[0:L, XT, c * P:(c + 1) * P], xbc[i][:, c, seq], ident[:])
                last.then_inc(pe_xt, 1)
                if head:
                    head_half(g + 1, 1)
                with_part(a_part, lambda: None if first else out(n - 1, 1 - j), lambda: mix_tokens(n, j))

            pipeline(pe, stage_a_head, stage_a, stage_b, lambda: out(SEQS - 1, 1))

        @block.scalar
        def _(act):
            act.wait_ge(w_loaded, 16 * WEIGHTS)
            act.activation(a_neg[:], a_neg[:], ACT.Exp).then_inc(a_ready, 1)
            act.wait_ge(prep, PREP)

            def stage_a_head(g):
                for k in range(KD):
                    act.wait_ge(pe_norm_t, KD * g + k + 1)
                    last = act.activation(u_t[:, k, :], psum[:, PROJ + 1 - k, 0:GL], ACT.Identity,
                                          scale=ln_w[:, k:k + 1], bias=ln_b[:, k:k + 1])
                last.then_inc(act_u, 1)

            def conv_tanh(g, k):
                e = nth("conv", k)
                act.wait_ge(proj_used, g * PRODUCTS + k + 1)
                act.activation(tanh[:, e % 2, :], acc[:, e % 2, :], ACT.Tanh, scale=0.5).then_inc(act_tanh, 1)

            def stage_a(g, i, part, hooks=()):
                for k in PARTS[part]:
                    if k == PARTS[part][-1] and PRODUCT[k - 1][0] == "conv":
                        conv_tanh(g, k - 1)
                    call_hooks(hooks, part, k)
                    kind, c = PRODUCT[k]
                    e = nth(kind, k)
                    if kind == "dt":
                        act.wait_ge(v_chain, g * CHAIN + 1)
                        act.activation(dt_e[:], dt_z[:], ACT.Exp).then_inc(act_dt, 1)
                    if kind == "conv":
                        if not (type(g) is int and g == 0) or e >= 2:
                            act.wait_ge(v_xbc, g * KC + e - 1)
                        act.wait_ge(pe_proj, g * PRODUCTS + k + 1)
                        act.activation(acc[:, e % 2, :], proj(k), ACT.Identity, scale=conv_w[:, c, TAPS - 1:TAPS],
                                       bias=conv_b[:, c:c + 1]).then_inc(act_tap, 1)
                    if kind == "gate":
                        act.wait_ge(pe_proj, g * PRODUCTS + k + 1)
                        if e >= 2:
                            act.wait_ge(proj_used, g * PRODUCTS + PRODUCT.index(("gate", e - 2)) + 1)
                        act.activation(tanh_z[:, e % 2, :], proj(k), ACT.Tanh, scale=0.5).then_inc(act_zt, 1)
                    if k and PRODUCT[k - 1][0] == "conv" and k != PARTS[part][-1]:
                        conv_tanh(g, k - 1)

            def square(n, j):
                act.wait_ge(v_gated, n + 1)
                if not (type(n) is int and n == 0):
                    act.wait_ge(p_half, n)
                act.activation(squares[:], gated[j][:], ACT.Square).then_inc(act_sq, 1)

            def stage_b(g, i, q, a_part, final):
                n, j = g * GROUP + q, q % 2
                act.wait_ge(pe_decay, n + 1)
                if not (type(n) is int and n < 2):
                    act.wait_ge(p_mix, n - 1)
                act.activation(decay[j][:].rearrange("p (a b) l -> p a (b l)", a=2), psum[0:L, DECAY:DECAY + 2, 0:GL],
                               ACT.Exp).then_inc(act_decay, 1)
                if q == 0 and a_part:
                    stage_a_head(g + 1)
                with_part(a_part, lambda: None, lambda: square(n, j))

            pipeline(act, stage_a_head, stage_a, stage_b, lambda: None)

        @block.gpsimd
        def _(pool):
            pool.wait_ge(w_loaded, 16 * WEIGHTS)
            pool.wait_ge(prep, PREP)

            def make_steps(n, i, q):
                j = q % 2
                if not (type(n) is int and n < 2):
                    pool.wait_ge(pe_decay, n - 1)
                pool.tensor_tensor(steps[j][:], bc_mid(upto[:], HEADS), bc_last(dt_a[i][:, q, :], L),
                                   ALU.mult).then_inc(p_steps, 1)

            def power(g):
                pool.wait_ge(v_var, g + 1)
                pool.tensor_tensor(rstd[:], var_eps[:], neg_half[:].rearrange("p (a b) -> p a b", a=2),
                                   ALU.pow).then_inc(p_rstd, 1)

            def skips(g, i, c):
                pool.wait_ge(v_xbc, g * KC + 2 + c + 2)
                pool.tensor_tensor(skip[i][:, c:c + 2, :], xbc[i][:, c:c + 2, :], bc_last(d_skip[:, c:c + 2], GL),
                                   ALU.mult).then_inc(p_skip, 1)

            def stage_a(g, i, part, hooks=()):
                if part == 3 and type(g) is int and g == 0:
                    pool.wait_ge(v_dt, 1)
                    make_steps(0, 0, 0)
                if part == 1 and not (type(g) is int and g == GROUPS - 1):
                    power(g + 1)
                if part == 3:
                    skips(g, i, 0)

            def power_rms(n):
                pool.wait_ge(v_ms, n + 1)
                pool.tensor_tensor(rms[:], ms[:], neg_half[:, 0:1], ALU.pow).then_inc(p_rms, 1)

            def stage_b(g, i, q, a_part, final):
                n, j = g * GROUP + q, q % 2
                pool.wait_ge(act_decay, n + 1)
                pool.wait_ge(v_cb, n + 1)
                pool.tensor_tensor(mix[j][:], decay[j][:], bc_mid(cb[j][:], HEADS), ALU.mult).then_inc(p_mix, 1)
                if not final:
                    if q == GROUP - 1:
                        pool.wait_ge(v_dt, g + 2)
                        make_steps(n + 1, 1 - i, 0)
                    else:
                        make_steps(n + 1, i, q + 1)
                if a_part:
                    a_part()
                if q == 0:
                    skips(g, i, 2)
                if not (type(n) is int and n == 0):
                    power_rms(n - 1)
                sum_squares(n)

            def sum_squares(n):
                pool.wait_ge(act_sq, n + 1)
                pool.tensor_tensor(sq_half[:], squares[:, 0:2, :], squares[:, 2:4, :], ALU.add).then_inc(p_half, 1)
                pool.wait_ge(p_half, n + 1)
                if not (type(n) is int and n == 0):
                    pool.wait_ge(pe_out, n)
                pool.tensor_tensor(sq_sum[:], sq_half[:, 0, :], sq_half[:, 1, :], ALU.add).then_inc(p_sum, 1)

            pipeline(pool, power, stage_a, stage_b, lambda: power_rms(SEQS - 1))

        @block.vector
        def _(dve):
            dve.wait_ge(w_loaded, 16 * WEIGHTS)
            dve.memset(neg_half[:], -0.5).then_inc(prep, 1)
            for c in range(KX):
                dve.tensor_scalar(w_out[:, c, :], w_out[:, c, :], gamma[:, c:c + 1], None, ALU.mult).then_inc(prep, 1)
            dve.tensor_scalar(d_skip[:], d_skip[:], 0.5, None, ALU.mult).then_inc(prep, 1)
            dve.wait_ge(a_ready, 1)
            dve.tensor_scalar(a_neg[:], a_neg[:], -1.0, None, ALU.mult).then_inc(prep, 1)
            dve.wait_ge(prep, PREP)

            def norm_statistics(g):
                dve.wait_ge(x_loaded, (g + 1) * 16)
                for b in range(GROUP):
                    last = dve.bn_stats(stats[:, b, :], x_res[:, g * GROUP + b, :])
                last.then_inc(v_stats, 1)
                wait_before(dve, idle[0:L, :], [(v_stats, g + 1)])
                for b in range(GROUP):
                    last = dve.bn_aggr(mean_var[:, b, :], stats[:, b, :])
                last.then_inc(v_aggr, 1)
                dve.wait_ge(v_aggr, g + 1)
                dve.tensor_scalar(var_eps[:, 0, :], mean_var[:, :, 1], EPS, None, ALU.add)
                dve.tensor_scalar(var_eps[:, 1, :], mean_var[:, :, 1], 1.0 + EPS, EPS * EPS, ALU.mult,
                                  ALU.add).then_inc(v_var, 1)

            def normalize(g):
                dve.wait_ge(p_rstd, g + 1)
                dve.tensor_scalar(res_scale[:], rstd[:, 0, :], 1.0, None, ALU.add)
                dve.scalar_tensor_tensor(res_shift[:], mean_var[:, :, 0], -1.0, rstd[:, 0, :], ALU.mult,
                                         ALU.mult).then_inc(v_res, 1)
                if not (type(g) is int and g == 0):
                    dve.wait_ge(pe_norm_t, KD * g)
                for b in range(GROUP):
                    last = dve.tensor_scalar(normed[:, b, :], x_res[:, g * GROUP + b, :], mean_var[:, b, 0:1],
                                             rstd[:, 1, b:b + 1], ALU.subtract, ALU.mult)
                last.then_inc(v_norm, 1)
                dve.wait_ge(v_res, g + 1)
                for b in range(GROUP):
                    dve.tensor_scalar(x_res[:, g * GROUP + b, :], x_res[:, g * GROUP + b, :], res_scale[:, b:b + 1],
                                      res_shift[:, b:b + 1], ALU.mult, ALU.add)

            def taps(g, k, e, c):
                a, src = by_seq(acc[:, e % 2, :]), by_seq(proj(k))
                dve.wait_ge(act_tap, g * KC + e + 1)
                for back in range(1, TAPS):
                    if back > 1:
                        dve.wait_ge(v_tap, (g * KC + e) * 2 + back - 1)
                    dve.scalar_tensor_tensor(a[:, :, back:], src[:, :, 0:L - back],
                                             conv_w[:, c, TAPS - 1 - back:TAPS - back], a[:, :, back:],
                                             ALU.mult, ALU.add).then_inc(v_tap if back < TAPS - 1 else proj_used, 1)

            def silu(g, i, e, c):
                dve.wait_ge(act_tanh, g * KC + e + 1)
                dve.scalar_tensor_tensor(xbc[i][:, c, :], tanh[:, e % 2, :], 1.0, acc[:, e % 2, :],
                                         ALU.add, ALU.mult).then_inc(v_xbc, 1)

            def dt_start(g):
                dve.wait_ge(pe_proj, g * PRODUCTS + 1)
                dve.tensor_tensor(dt_raw[:], psum[0:L, PROJ, 0:GROUP * HEADS].rearrange(
                    "p (b h) -> p b h", b=GROUP), bc_mid(dt_bias[:], GROUP), ALU.add).then_inc(proj_used, 1)
                dve.wait_ge(proj_used, g * PRODUCTS + 1)
                dve.scalar_tensor_tensor(dt_z[:], dt_raw[:], -1.0, dt_raw[:], ALU.mult, ALU.min).then_inc(v_chain, 1)

            def then(g, step, ins):
                ins.then_inc(v_chain, 1)
                dve.wait_ge(v_chain, g * CHAIN + step)

            def softplus_argument(g):
                dve.tensor_scalar(dt_raw[:], dt_raw[:], 0.0, None, ALU.max)
                dve.wait_ge(act_dt, g + 1)
                then(g, 2, dve.tensor_scalar(dt_p[:], dt_e[:], 2.0, None, ALU.add))
                then(g, 3, dve.reciprocal(dt_p[:], dt_p[:]))
                then(g, 4, dve.tensor_tensor(dt_z[:], dt_e[:], dt_p[:], ALU.mult))
                then(g, 5, dve.tensor_tensor(dt_z2[:], dt_z[:], dt_z[:], ALU.mult))
                then(g, 6, dve.tensor_scalar(dt_p[:], dt_z2[:], 1.0 / (2 * LOG_TERMS + 1), None, ALU.mult))

            def softplus_series(g, i):
                for m in range(LOG_TERMS - 1, 0, -1):
                    then(g, 6 + LOG_TERMS - m, dve.scalar_tensor_tensor(
                        dt_p[:], dt_p[:], 1.0 / (2 * m + 1), dt_z2[:], ALU.add, ALU.mult))
                last = 5 + LOG_TERMS
                then(g, last + 1, dve.scalar_tensor_tensor(dt_p[:], dt_p[:], 1.0, dt_z[:], ALU.add, ALU.mult))
                then(g, last + 2, dve.scalar_tensor_tensor(dt_raw[:], dt_p[:], 2.0, dt_raw[:], ALU.mult, ALU.add))
                dve.tensor_scalar(dt_8[i][:], dt_raw[:], 0.125, None, ALU.mult)
                dve.tensor_tensor(dt_a[i][:], dt_raw[:], bc_mid(a_neg[:], GROUP), ALU.mult).then_inc(v_dt, 1)
                assert last + 2 == CHAIN

            def stage_a(g, i, part, hooks=()):
                more = not (type(g) is int and g == GROUPS - 1)
                if part == 0 and more:
                    norm_statistics(g + 1)
                if part == 1:
                    softplus_argument(g)
                if part == 2:
                    softplus_series(g, i)
                if part == 3 and more:
                    normalize(g + 1)
                for k in PARTS[part]:
                    kind, c = PRODUCT[k]
                    e = nth(kind, k)
                    call_hooks(hooks, part, k)
                    last = k == PARTS[part][-1]
                    silu_due = k and PRODUCT[k - 1][0] == "conv"
                    if silu_due and last:
                        silu(g, i, nth("conv", k - 1), PRODUCT[k - 1][1])
                    if kind == "dt":
                        dt_start(g)
                    if kind == "conv":
                        taps(g, k, e, c)
                    if kind == "gate":
                        dve.wait_ge(act_zt, g * KX + e + 1)
                        dve.scalar_tensor_tensor(gate[i][:, c, :], tanh_z[:, e % 2, :], 1.0, proj(k),
                                                 ALU.add, ALU.mult).then_inc(proj_used, 1)
                    if silu_due and not last:
                        silu(g, i, nth("conv", k - 1), PRODUCT[k - 1][1])

            def stage_a_head(g):
                norm_statistics(g)
                normalize(g)

            def residual(n):
                dve.wait_ge(p_rms, n + 1)
                dve.scalar_tensor_tensor(x_res[:, n, :], psum[0:L, OUT, 0:D], rms[:, 0:1], x_res[:, n, :],
                                         ALU.mult, ALU.add).then_inc(v_x1, 1)

            def mean_square(n):
                dve.wait_ge(pe_out, n + 1)
                dve.tensor_scalar(ms[:], psum[0:L, OUT, D:D + 1], 1.0 / INNER, 4 * EPS, ALU.mult,
                                  ALU.add).then_inc(v_ms, 1)

            def gate_tokens(n, g, i, q):
                j, seq = q % 2, slice(q * L, (q + 1) * L)
                dve.wait_ge(pe_y, n + 1)
                dve.wait_ge(p_skip, 2 * (g + 1))
                dve.tensor_tensor(y_skip[j][:], psum[:, Y, 0:GL].rearrange("p (c l) -> p c l", c=KX),
                                  skip[i][:, :, seq], ALU.add).then_inc(v_yskip, 1)
                dve.wait_ge(v_yskip, n + 1)
                dve.tensor_tensor(gated[j][:], y_skip[j][:], gate[i][:, :, seq], ALU.mult).then_inc(v_gated, 1)
                if not (type(n) is int and n == 0):
                    residual(n - 1)

            def stage_b(g, i, q, a_part, final):
                n, j = g * GROUP + q, q % 2
                first = type(n) is int and n == 0
                dve.wait_ge(pe_cb, n + 1)
                dve.tensor_tensor(cb[j][:], psum[0:L, CB, 0:L], upto[:], ALU.mult).then_inc(v_cb, 1)
                dve.wait_ge(pe_xt, n + 1)
                dve.tensor_tensor(x_dt[j][:], psum[0:L, XT, :].rearrange("p (h c) -> p h c", h=HEADS),
                                  bc_last(dt_8[i][:, q, :], HEADDIM), ALU.mult).then_inc(v_xdt, 1)
                with_part(a_part, lambda: None if first else mean_square(n - 1), lambda: gate_tokens(n, g, i, q))

            def tail():
                mean_square(SEQS - 1)
                residual(SEQS - 1)

            pipeline(dve, stage_a_head, stage_a, stage_b, tail)


C = 361
CP = C + 1
NH, DK = 16, 16
ROWS = [(0, 121), (121, 121), (242, 119)]
HG = 4
NG = NH // HG
VW = 32
MASKED = -1e30


def cross_block(nc, x_res, x_out, t):
    with ExitStack() as ctx:
        def sb(name, shape, dt=F32):
            return ctx.enter_context(nc.sbuf_tensor(name, shape, dt))

        def pair(name, shape, dt=F32):
            return [sb(f"{name}{i}", shape, dt) for i in range(2)]

        def sem(name):
            return ctx.enter_context(nc.semaphore(name))

        wq = sb("wq", [P, KD, D])
        wo = sb("wo", [P, KD, D])
        w_raw = sb("w_raw", [P, 2, KD, D])
        w_hi = sb("w_hi", [P, 2, KD, D], F32R)
        w_lo = sb("w_lo", [P, 2, KD, D], F32R)
        ident = sb("ident_c", [P, P])
        block8 = sb("block8", [P, 8])
        mask_raw = sb("mask_raw", [NH + L, C], I32)
        mask_row = sb("mask_row", [L, C], I32)
        bias_row = sb("bias_row", [L, CP])
        shift_w = sb("shift_w", [NH + L, NG, C], F32R)
        pick_raw = sb("pick_raw", [NH, NG])
        place = sb("place", [NH, HG])
        shift_raw = sb("shift_raw", [NH + L, HG * L])
        shift = pair("shift", [NH + L, HG * L], F32R)
        any_row = sb("any_row", [L, 1])
        any_inv = sb("any_inv", [L, 1])
        keep_row = sb("keep_row", [L, 1])
        neg_half = sb("neg_half_c", [L, 1])

        ctx_raw = pair("ctx_raw", [P, KD, CP])
        ctx_hi = pair("ctx_hi", [P, KD, CP], F32R)
        ctx_lo = pair("ctx_lo", [P, KD, CP], F32R)
        stats = sb("stats_c", [L, 6])
        mean_var = sb("mean_var_c", [L, 2])
        var_eps = sb("var_eps_c", [L, 1])
        rstd = sb("rstd_c", [L, 1])
        normed = pair("normed_c", [L, D])
        norm_t = sb("norm_t", [P, KD, L])
        q_hi = sb("q_hi", [P, KD, L], F32R)
        q_lo = sb("q_lo", [P, KD, L])
        qb_hi = pair("qb_hi", [P, NG, HG * L], F32R)
        qb_lo = pair("qb_lo", [P, NG, HG * L], F32R)
        k_hi = pair("k_hi", [P, KD, CP], F32R)
        k_lo = pair("k_lo", [P, KD, CP], F32R)
        val = pair("val", [P, len(ROWS), NH, VW])
        scored = pair("scored", [L, CP])
        row_max = sb("row_max", [L, NH])
        probs = pair("probs", [P, len(ROWS), 2 * HG * L])
        o_t = sb("o_t", [P, NG, L])
        rden = sb("rden", [L, NH])
        o_n = sb("o_n", [L, NH, DK])
        on_t = sb("on_t", [P, KD, L])
        x2 = pair("x2", [L, D])
        idle = sb("idle_c", [L, 1 + NH])

        psum = ctx.enter_context(nc.psum_tensor("psum_c", [P, 8, 512], F32))
        SCORE, O, KV, MISC = 0, 4, 5, 7

        w_loaded = sem("c_w_loaded")
        ready = sem("c_ready")
        prep = sem("c_prep")
        ctx_in = [sem(f"ctx_in{i}") for i in range(2)]
        x2_out = [sem(f"x2_out{i}") for i in range(2)]
        act_chi = sem("act_chi")
        p_clo = sem("p_clo")
        v_ln = sem("v_ln")
        v_var = sem("c_v_var")
        p_rstd = sem("c_p_rstd")
        v_norm = sem("c_v_norm")
        pe_nt = sem("pe_nt")
        act_nt = sem("act_nt")
        pe_q = sem("pe_q")
        v_qhi = sem("v_qhi")
        v_q = sem("v_q")
        p_qb = sem("p_qb")
        pe_k = sem("pe_k")
        act_khi = sem("act_khi")
        v_klo = sem("v_klo")
        pe_v = sem("pe_v")
        act_v = sem("act_v")
        pe_max = sem("pe_max")
        v_max = sem("v_max")
        pe_maxt = sem("pe_maxt")
        v_shift = sem("v_shift")
        pe_score = sem("pe_score")
        act_exp = sem("act_exp")
        pe_pv = sem("pe_pv")
        act_o = sem("act_o")
        pe_ot = sem("pe_ot")
        v_rden = sem("v_rden")
        v_on = sem("v_on")
        pe_ont = sem("pe_ont")
        act_ont = sem("act_ont")
        pe_wo = sem("pe_wo")
        v_x2 = sem("v_x2")

        WEIGHTS = 12
        STEPS = 2 * len(ROWS)
        NC = len(ROWS)

        def after(m, p, k):
            return m + (p + k) // 2, (p + k) % 2

        def at(m, p):
            return 2 * m + p

        def pipeline(eng, prologue, sequence):
            prologue()
            sequence(0, 0)
            sequence(0, 1)
            with eng.Fori(1, SEQS // 2 - 2) as m:
                sequence(m, 0)
                sequence(m, 1)
            for m in range(SEQS // 2 - 2, SEQS // 2):
                sequence(m, 0)
                sequence(m, 1)

        def has(m, p, k):
            return type(m) is not int or 0 <= 2 * m + p + k < SEQS

        block = ctx.enter_context(nc.Block())

        @block.sync
        def _(sp):
            def load(m, p):
                sp.dma_start(ctx_raw[p][:, :, 0:C], t["ctx_t"][at(m, p)].rearrange("(k q) c -> q k c", q=P)
                             ).then_inc(ctx_in[p], 16)

            loads = [
                (w_raw[:, 0], t["wk"].rearrange("(k p) n -> p k n", p=P)),
                (w_raw[:, 1], t["wv"].rearrange("(k p) n -> p k n", p=P)),
                (wq[:], t["wq"].rearrange("(k p) n -> p k n", p=P)),
                (ident[:], t["ident"]), (block8[:], t["block8"]),
                (mask_raw[0:NH, :], t["mask"][0:NH, :]), (mask_raw[NH:NH + L, :], t["mask"]), (mask_row[:], t["mask"]),
                (pick_raw[:], t["pick"]), (place[:], t["place"]), (shift_raw[:], t["shift"]),
                (wo[:], t["wo"].rearrange("(k p) n -> p k n", p=P)),
            ]
            for dst, src in loads:
                sp.dma_start(dst, src).then_inc(w_loaded, 16)
            load(0, 0)
            load(0, 1)
            sp.wait_ge(act_chi, 1)
            sp.wait_ge(p_clo, 1)
            load(1, 0)

            def sequence(m, p):
                if has(m, p, 3):
                    m1, p1 = after(m, p, 1)
                    sp.wait_ge(act_chi, at(m1, p1) + 1)
                    sp.wait_ge(p_clo, at(m1, p1) + 1)
                    load(*after(m, p, 3))
                if has(m, p, -1):
                    mb, pb = after(m, p, -1)
                    sp.wait_ge(v_x2, at(mb, pb) + 1)
                    sp.dma_start(x_out[at(mb, pb)], x2[pb][:]).then_inc(x2_out[pb], 16)

            pipeline(sp, lambda: None, sequence)
            sp.wait_ge(v_x2, SEQS)
            sp.dma_start(x_out[SEQS - 1], x2[1][:]).then_inc(x2_out[1], 16)
            for p in range(2):
                sp.wait_ge(x2_out[p], 16 * SEQS // 2)

        @block.tensor
        def _(pe):
            pe.wait_ge(prep, 1)

            def split_product(out, a_hi, a_lo, b_hi, b_lo, start, stop):
                pe.matmul(out, a_hi, b_hi, start=start, stop=False)
                pe.matmul(out, a_lo, b_hi, start=False, stop=False)
                return pe.matmul(out, a_hi, b_lo, start=False, stop=stop)

            def norm_transposes(m, p):
                n = at(m, p)
                pe.wait_ge(v_norm, n + 1)
                if has(m, p, -1):
                    pe.wait_ge(v_shift, n)
                for k in range(KD):
                    last = pe.transpose(psum[:, MISC, k * L:(k + 1) * L], normed[p][:, k * P:(k + 1) * P],
                                        ident[0:L, 0:L])
                last.then_inc(pe_nt, 1)

            def project_q(m, p):
                pe.wait_ge(act_nt, at(m, p) + 1)
                for k in range(KD):
                    for d in range(KD):
                        last = pe.matmul(psum[:, MISC, k * L:(k + 1) * L], wq[:, d, k * P:(k + 1) * P],
                                         norm_t[:, d, :], start=d == 0, stop=d == KD - 1)
                last.then_inc(pe_q, 1)

            def project_k(m, p):
                n = at(m, p)
                pe.wait_ge(p_clo, n + 1)
                if has(m, p, -1):
                    pe.wait_ge(v_max, n * NH)
                for k in range(KD):
                    cols = slice(k * P, (k + 1) * P)
                    for d in range(KD):
                        last = split_product(psum[:, KV + k, 0:CP], w_hi[:, 0, d, cols], w_lo[:, 0, d, cols],
                                             ctx_hi[p][:, d, :], ctx_lo[p][:, d, :], d == 0, d == KD - 1)
                    last.then_inc(pe_k, 1)

            def project_v(m, p, c):
                n = at(m, p)
                if c < 2:
                    pe.wait_ge(v_klo, KD * n + c + 1)
                else:
                    pe.wait_ge(act_v, NC * n + 1)
                start, rows = ROWS[c]
                for d in range(KD):
                    last = split_product(psum[0:rows, KV + c % 2, 0:D], ctx_hi[p][:, d, start:start + rows],
                                         ctx_lo[p][:, d, start:start + rows], w_hi[:, 1, d, :], w_lo[:, 1, d, :],
                                         d == 0, d == KD - 1)
                last.then_inc(pe_v, 1)

            def max_scores(m, p, heads):
                n = at(m, p)
                for h in heads:
                    if h % 8 == 0:
                        pe.wait_ge(p_qb, 4 * n + 1 + h // 8)
                    if h == 0:
                        pe.wait_ge(v_klo, KD * (n + 1))
                    if h < 2:
                        pe.wait_ge(act_v, NC * n + 2 + h)
                    else:
                        pe.wait_ge(v_max, NH * n + h - 1)
                    g, j = h // HG, h % HG
                    pe.matmul(psum[0:L, KV + (h + 1) % 2, 0:CP], qb_hi[p][:, g, j * L:(j + 1) * L],
                              k_hi[p][:, g // 2, :], start=True, stop=True).then_inc(pe_max, 1)

            def max_transpose(m, p):
                n = at(m, p)
                pe.wait_ge(v_max, NH * (n + 1))
                if has(m, p, -2):
                    pe.wait_ge(v_x2, n - 1)
                elif has(m, p, -1):
                    pe.wait_ge(v_q, n + 1)
                else:
                    pe.wait_ge(v_q, 1)
                pe.transpose(psum[0:NH, MISC, 0:L], row_max[:], ident[0:L, 0:L]).then_inc(pe_maxt, 1)

            def scores(m, p, i):
                n = at(m, p)
                pr, c = i // NC, i % NC
                start, rows = ROWS[c]
                if i == 0:
                    pe.wait_ge(v_shift, n + 1)
                    pe.wait_ge(p_qb, 4 * n + 4)
                if not (type(m) is int and n == 0 and i < 2):
                    pe.wait_ge(act_exp, STEPS * n + i - 1)
                for half in range(2):
                    g = 2 * pr + half
                    out = psum[0:rows, SCORE + 2 * (i % 2) + half, 0:HG * L]
                    cols = slice(start, start + rows)
                    pe.matmul(out, shift_w[:, g, cols], shift[p][:], start=True, stop=False)
                    last = split_product(out, k_hi[p][:, pr, cols], k_lo[p][:, pr, cols], qb_hi[p][:, g, :],
                                         qb_lo[p][:, g, :], False, True)
                last.then_inc(pe_score, 1)

            def mix_values(m, p, g):
                n = at(m, p)
                pe.wait_ge(act_exp, STEPS * n + NC * (g // 2 + 1))
                if g == 0:
                    pe.wait_ge(act_v, NC * (n + 1))
                    if has(m, p, -1):
                        pe.wait_ge(act_o, n)
                for j in range(HG):
                    for c in range(NC):
                        rows = ROWS[c][1]
                        at_col = ((g % 2) * HG + j) * L
                        last = pe.matmul(psum[VW * j:VW * (j + 1), O, g * L:(g + 1) * L],
                                         val[p][0:rows, c, HG * g + j, :],
                                         probs[g // 2][0:rows, c, at_col:at_col + L], start=c == 0, stop=c == NC - 1)
                if g % 2:
                    last.then_inc(pe_pv, 1)

            def o_transposes(m, p, fresh):
                n = at(m, p)
                pe.wait_ge(act_o, n + 1)
                if fresh:
                    pe.wait_ge(v_q, n + 3)
                else:
                    pe.wait_ge(v_shift, SEQS)
                    if n == SEQS - 1:
                        pe.wait_ge(v_x2, SEQS - 1)
                for g in range(NG):
                    last = pe.transpose(psum[0:L, MISC, g * P:(g + 1) * P], o_t[:, g, :], ident[:])
                last.then_inc(pe_ot, 1)

            def on_transposes(m, p):
                pe.wait_ge(v_on, at(m, p) + 1)
                for k in range(KD):
                    last = pe.transpose(psum[:, MISC, k * L:(k + 1) * L],
                                        o_n[:].rearrange("l h d -> l (h d)")[:, k * P:(k + 1) * P], ident[0:L, 0:L])
                last.then_inc(pe_ont, 1)

            def project_out(m, p):
                pe.wait_ge(act_ont, at(m, p) + 1)
                for k in range(KD):
                    last = pe.matmul(psum[0:L, MISC, 0:D], on_t[:, k, :], wo[:, k, :], start=k == 0, stop=k == KD - 1)
                last.then_inc(pe_wo, 1)

            def prologue():
                norm_transposes(0, 0)
                project_k(0, 0)
                project_q(0, 0)
                for c in range(NC):
                    project_v(0, 0, c)
                max_scores(0, 0, range(NH))
                max_transpose(0, 0)

            def sequence(m, p):
                nxt = after(m, p, 1) if has(m, p, 1) else None
                prv = after(m, p, -1) if has(m, p, -1) else None
                if nxt:
                    project_k(*nxt)
                    norm_transposes(*nxt)
                scores(m, p, 0)
                if nxt:
                    project_q(*nxt)
                scores(m, p, 1)
                if nxt:
                    project_v(*nxt, 0)
                    project_v(*nxt, 1)
                scores(m, p, 2)
                if nxt:
                    project_v(*nxt, 2)
                if prv:
                    o_transposes(*prv, bool(nxt))
                def pair_of_heads(i):
                    if nxt:
                        max_scores(*nxt, range(2 * i, 2 * i + 2))
                pair_of_heads(0)
                scores(m, p, 3)
                pair_of_heads(1)
                mix_values(m, p, 0)
                pair_of_heads(2)
                mix_values(m, p, 1)
                pair_of_heads(3)
                if prv:
                    on_transposes(*prv)
                scores(m, p, 4)
                pair_of_heads(4)
                scores(m, p, 5)
                pair_of_heads(5)
                if prv:
                    project_out(*prv)
                pair_of_heads(6)
                mix_values(m, p, 2)
                pair_of_heads(7)
                mix_values(m, p, 3)
                if nxt:
                    max_transpose(*nxt)

            pipeline(pe, prologue, sequence)
            last = (SEQS // 2 - 1, 1)
            o_transposes(*last, False)
            on_transposes(*last)
            project_out(*last)

        @block.scalar
        def _(act):
            act.wait_ge(prep, 1)

            def split_context(m, p):
                act.wait_ge(ctx_in[p], 16 * (m + 1))
                if has(m, p, -2):
                    act.wait_ge(pe_v, NC * (at(m, p) - 1))
                act.copy(ctx_hi[p][:], ctx_raw[p][:]).then_inc(act_chi, 1)

            def norm_copy(m, p):
                act.wait_ge(pe_nt, at(m, p) + 1)
                act.copy(norm_t[:], psum[:, MISC, 0:KD * L].rearrange("p (k l) -> p k l", k=KD)).then_inc(act_nt, 1)

            def key_copy(m, p):
                for k in range(KD):
                    act.wait_ge(pe_k, KD * at(m, p) + k + 1)
                    act.copy(k_hi[p][:, k, :], psum[:, KV + k, 0:CP]).then_inc(act_khi, 1)

            def value_copy(m, p, c):
                act.wait_ge(pe_v, NC * at(m, p) + c + 1)
                rows = ROWS[c][1]
                act.copy(val[p][0:rows, c, :, 0:DK], psum[0:rows, KV + c % 2, 0:D].rearrange(
                    "p (h d) -> p h d", h=NH)).then_inc(act_v, 1)

            def exps(m, p, i):
                n = at(m, p)
                pr, c = i // NC, i % NC
                rows = ROWS[c][1]
                act.wait_ge(pe_score, STEPS * n + i + 1)
                if c == 0 and has(m, p, -1):
                    act.wait_ge(pe_pv, 2 * n - 1 + pr)
                act.activation(probs[pr][0:rows, c, :].rearrange("p (a b) -> p a b", a=2),
                               psum[0:rows, SCORE + 2 * (i % 2):SCORE + 2 * (i % 2) + 2, 0:HG * L],
                               ACT.Exp).then_inc(act_exp, 1)

            def o_copy(m, p):
                n = at(m, p)
                act.wait_ge(pe_pv, 2 * (n + 1))
                if has(m, p, -1):
                    act.wait_ge(pe_ot, n)
                act.copy(o_t[:], psum[:, O, 0:NG * L].rearrange("p (g l) -> p g l", g=NG)).then_inc(act_o, 1)

            def on_copy(m, p):
                n = at(m, p)
                act.wait_ge(pe_ont, n + 1)
                act.copy(on_t[:], psum[:, MISC, 0:KD * L].rearrange("p (k l) -> p k l", k=KD)).then_inc(act_ont, 1)

            def prologue():
                split_context(0, 0)
                norm_copy(0, 0)
                key_copy(0, 0)
                for c in range(NC):
                    value_copy(0, 0, c)
                split_context(0, 1)

            def sequence(m, p):
                nxt = after(m, p, 1) if has(m, p, 1) else None
                prv = after(m, p, -1) if has(m, p, -1) else None
                if nxt:
                    key_copy(*nxt)
                    norm_copy(*nxt)
                exps(m, p, 0)
                exps(m, p, 1)
                if nxt:
                    value_copy(*nxt, 0)
                    value_copy(*nxt, 1)
                exps(m, p, 2)
                if nxt:
                    value_copy(*nxt, 2)
                if has(m, p, 2):
                    split_context(*after(m, p, 2))
                exps(m, p, 3)
                if prv:
                    on_copy(*prv)
                exps(m, p, 4)
                exps(m, p, 5)
                o_copy(m, p)

            pipeline(act, prologue, sequence)
            on_copy(SEQS // 2 - 1, 1)

        @block.gpsimd
        def _(pool):
            pool.wait_ge(prep, 1)

            def split_context(m, p):
                n = at(m, p)
                pool.wait_ge(act_chi, n + 1)
                pool.tensor_tensor(ctx_lo[p][:], ctx_raw[p][:], ctx_hi[p][:].bitcast(F32), ALU.subtract
                                   ).then_inc(p_clo, 1)

            def block_queries(m, p):
                n = at(m, p)
                pool.wait_ge(v_q, n + 1)
                if has(m, p, -2):
                    pool.wait_ge(pe_score, STEPS * (n - 1))
                for src, dst in ((q_hi, qb_hi), (q_lo, qb_lo)):
                    for k in range(KD):
                        row = src[:, k, :]
                        if src is q_hi:
                            row = row.bitcast(F32)
                        pool.tensor_tensor(dst[p][:, 2 * k:2 * k + 2, :].rearrange("p g (j l) -> p (g j) l", l=L),
                                           bc_mid(row, 8), bc_last(block8[:], L), ALU.mult).then_inc(p_qb, 1)

            def power(m, p):
                pool.wait_ge(v_var, at(m, p) + 1)
                pool.tensor_tensor(rstd[:], var_eps[:], neg_half[:], ALU.pow).then_inc(p_rstd, 1)

            def prologue():
                power(0, 0)
                split_context(0, 0)
                block_queries(0, 0)
                power(0, 1)
                split_context(0, 1)

            def sequence(m, p):
                if has(m, p, 1):
                    block_queries(*after(m, p, 1))
                if has(m, p, 2):
                    power(*after(m, p, 2))
                    split_context(*after(m, p, 2))

            pipeline(pool, prologue, sequence)

        @block.vector
        def _(dve):
            dve.wait_ge(w_loaded, 16 * WEIGHTS)
            chain = [0]

            def then(ins):
                chain[0] += 1
                ins.then_inc(ready, 1)
                dve.wait_ge(ready, chain[0])

            then(dve.memset(neg_half[:], -0.5))
            then(dve.tensor_copy(w_hi[:], w_raw[:]))
            then(dve.tensor_tensor(w_lo[:], w_raw[:], w_hi[:].bitcast(F32), ALU.subtract))
            then(dve.memset(bias_row[:], MASKED))
            then(dve.tensor_scalar(bias_row[:, 0:C], mask_row[:], 0.0, MASKED, ALU.is_equal, ALU.mult))
            for g in range(NG):
                then(dve.tensor_scalar(shift_w[:, g, :], mask_raw[:], 0.0, MASKED, ALU.is_equal, ALU.mult))
                then(dve.tensor_copy(shift_w[0:NH, g, :], pick_raw[:, g:g + 1].to_broadcast([NH, C])))
            then(dve.tensor_reduce(any_row[:], bias_row[:], AX.X, ALU.max))
            then(dve.tensor_scalar(any_row[:], any_row[:], 0.0, None, ALU.is_equal))
            then(dve.reciprocal(any_inv[:], any_row[:]))
            then(dve.tensor_tensor(keep_row[:], any_row[:], any_inv[:], ALU.mult))
            for p in range(2):
                then(dve.memset(ctx_raw[p][:, :, C:CP], 0.0))
                then(dve.tensor_copy(shift[p][:], shift_raw[:]))
                then(dve.memset(val[p][:], 0.0))
                then(dve.memset(val[p][:, :, :, DK:DK + 1], 1.0))
            dve.tensor_copy(any_inv[:], any_row[:]).then_inc(prep, 1)

            def statistics(m, p):
                n = at(m, p)
                dve.bn_stats(stats[:], x_res[:, n, :]).then_inc(v_ln, 1)
                wait_before(dve, idle[:, 0:1], [(v_ln, 2 * n + 1)])
                dve.bn_aggr(mean_var[:], stats[:]).then_inc(v_ln, 1)
                dve.wait_ge(v_ln, 2 * n + 2)
                dve.tensor_scalar(var_eps[:], mean_var[:, 1:2], EPS, None, ALU.add).then_inc(v_var, 1)

            def normalize(m, p):
                n = at(m, p)
                dve.wait_ge(p_rstd, n + 1)
                if has(m, p, -2):
                    dve.wait_ge(pe_nt, n - 1)
                dve.tensor_scalar(normed[p][:], x_res[:, n, :], mean_var[:, 0:1], rstd[:, 0:1], ALU.subtract,
                                  ALU.mult).then_inc(v_norm, 1)

            def key_low(m, p):
                for k in range(KD):
                    dve.wait_ge(act_khi, KD * at(m, p) + k + 1)
                    dve.tensor_tensor(k_lo[p][:, k, :], psum[:, KV + k, 0:CP], k_hi[p][:, k, :].bitcast(F32),
                                      ALU.subtract).then_inc(v_klo, 1)

            def queries(m, p):
                n = at(m, p)
                src = psum[:, MISC, 0:KD * L].rearrange("p (k l) -> p k l", k=KD)
                dve.wait_ge(pe_q, n + 1)
                if has(m, p, -1):
                    dve.wait_ge(p_qb, 4 * n)
                dve.tensor_scalar(q_hi[:], src, 0.25, None, ALU.mult).then_inc(v_qhi, 1)
                dve.wait_ge(v_qhi, n + 1)
                dve.scalar_tensor_tensor(q_lo[:], src, 0.25, q_hi[:].bitcast(F32), ALU.mult, ALU.subtract
                                         ).then_inc(v_q, 1)

            def maxima(m, p, heads):
                n = at(m, p)
                for h in heads:
                    waits = [(pe_max, NH * n + h + 1)]
                    if h > 1 or has(m, p, -1):
                        waits.append((v_max, NH * n + h - 1))
                    if h == 0 and has(m, p, -1):
                        waits.append((pe_maxt, n))
                    wait_before(dve, idle[:, 1 + h:2 + h], waits)
                    dve.tensor_tensor_reduce(out=scored[h % 2][:], in0=psum[0:L, KV + (h + 1) % 2, 0:CP], in1=bias_row[:],
                                             scale=1.0, scalar=-3e38, op0=ALU.add, op1=ALU.max,
                                             accum_out=row_max[:, h:h + 1]).then_inc(v_max, 1)

            def place_shift(m, p):
                n = at(m, p)
                dve.wait_ge(pe_maxt, n + 1)
                if has(m, p, -2):
                    dve.wait_ge(pe_score, STEPS * (n - 1))
                dve.tensor_tensor(shift[p][0:NH, :].rearrange("h (j l) -> h j l", j=HG),
                                  bc_mid(psum[0:NH, MISC, 0:L], HG), bc_last(place[:], L), ALU.mult
                                  ).then_inc(v_shift, 1)

            def normalize_o(m, p):
                n = at(m, p)
                src = psum[0:L, MISC, :].rearrange("l (h w) -> l h w", h=NH)
                dve.wait_ge(pe_ot, n + 1)
                dve.reciprocal(rden[:], src[:, :, DK]).then_inc(v_rden, 1)
                dve.wait_ge(v_rden, 2 * n + 1)
                dve.tensor_scalar(rden[:], rden[:], keep_row[:, 0:1], None, ALU.mult).then_inc(v_rden, 1)
                dve.wait_ge(v_rden, 2 * n + 2)
                dve.tensor_tensor(o_n[:], src[:, :, 0:DK], bc_last(rden[:], DK), ALU.mult).then_inc(v_on, 1)

            def residual(m, p):
                n = at(m, p)
                dve.wait_ge(pe_wo, n + 1)
                if has(m, p, -2):
                    dve.wait_ge(x2_out[p], 16 * m)
                dve.tensor_tensor(x2[p][:], psum[0:L, MISC, 0:D], x_res[:, n, :], ALU.add).then_inc(v_x2, 1)

            def prologue():
                statistics(0, 0)
                normalize(0, 0)
                key_low(0, 0)
                queries(0, 0)
                statistics(0, 1)
                normalize(0, 1)
                maxima(0, 0, range(NH))
                place_shift(0, 0)

            def sequence(m, p):
                nxt = after(m, p, 1) if has(m, p, 1) else None
                prv = after(m, p, -1) if has(m, p, -1) else None
                aft = after(m, p, 2) if has(m, p, 2) else None
                if nxt:
                    key_low(*nxt)
                    queries(*nxt)
                if prv:
                    normalize_o(*prv)
                if nxt:
                    maxima(*nxt, range(0, 4))
                if aft:
                    statistics(*aft)
                if nxt:
                    maxima(*nxt, range(4, 8))
                if aft:
                    normalize(*aft)
                if nxt:
                    maxima(*nxt, range(8, 12))
                if prv:
                    residual(*prv)
                if nxt:
                    maxima(*nxt, range(12, NH))
                    place_shift(*nxt)

            pipeline(dve, prologue, sequence)
            last = (SEQS // 2 - 1, 1)
            normalize_o(*last)
            residual(*last)


TOKENS = SEQS * L
TILES = 5
BLOCK = TILES * P
BLOCKS = TOKENS // BLOCK
HALF = BLOCK // 2
EXPERTS, HIDDEN = 8, 512
KH = HIDDEN // P


def moe_block(nc, x_in, out, t):
    with ExitStack() as ctx:
        def sb(name, shape, dt=F32):
            return ctx.enter_context(nc.sbuf_tensor(name, shape, dt))

        def pair(name, shape, dt=F32):
            return [sb(f"{name}{i}", shape, dt) for i in range(2)]

        def sem(name):
            return ctx.enter_context(nc.semaphore(name))

        w1_hi = sb("w1_hi", [P, EXPERTS, KD, HIDDEN], F32R)
        w1_lo = sb("w1_lo", [P, EXPERTS, KD, HIDDEN], F32R)
        w2_hi = sb("w2_hi", [P, EXPERTS, KH, D], F32R)
        w2_lo = sb("w2_lo", [P, EXPERTS, KH, D], F32R)
        w1_raw = sb("w1_raw", [P, KD, HIDDEN])
        w2_raw = sb("w2_raw", [P, KH, D])
        wg = sb("wg", [P, KD, EXPERTS])
        ident = sb("ident_f", [P, P])
        iota = sb("iota", [P, EXPERTS])
        neg_half = sb("neg_half_f", [P, TILES])

        y = sb("y", [P, BLOCKS, TILES, D])
        combine = sb("combine", [P, BLOCKS, TILES, EXPERTS])
        stats = sb("stats_f", [P, TILES, 6])
        mean_var = sb("mean_var_f", [P, TILES, 2])
        var_eps = sb("var_eps_f", [P, TILES])
        rstd = sb("rstd_f", [P, TILES])
        normed = sb("normed_f", [P, TILES, D])
        n_t = sb("n_t", [P, KD, BLOCK])
        x_hi = sb("x_hi", [P, KD, BLOCK], F32R)
        x_lo = sb("x_lo", [P, KD, BLOCK], F32R)
        gates = sb("gates", [P, TILES, EXPERTS])
        best = sb("best", [P, TILES, 8])
        best_at = sb("best_at", [P, TILES, 8], mybir.dt.uint32)
        best_f = sb("best_f", [P, TILES, 8])
        lead = sb("lead", [P, 2, TILES])
        share = sb("share", [P, 2, TILES])
        is_top = sb("is_top", [P, 2, TILES, EXPERTS])
        idle = sb("idle_f", [P, 3])
        h = pair("h", [P, BLOCK])
        h_hi = pair("h_hi", [P, BLOCK], F32R)
        h_lo = pair("h_lo", [P, BLOCK], F32R)

        psum = ctx.enter_context(nc.psum_tensor("psum_f", [P, 8, 512], F32))
        HID, Y, MISC = 0, 4, 7

        w_loaded = sem("f_w_loaded")
        prep = sem("f_prep")
        x_loaded = sem("f_x_loaded")
        w1_in = sem("w1_in")
        w2_in = sem("w2_in")
        v_w1hi = sem("v_w1hi")
        v_w1 = sem("v_w1")
        v_w2hi = sem("v_w2hi")
        v_w2 = sem("v_w2")
        v_ln = sem("f_v_ln")
        v_var = sem("f_v_var")
        p_rstd = sem("f_p_rstd")
        v_norm = sem("f_v_norm")
        pe_nt = sem("f_pe_nt")
        act_nt = sem("f_act_nt")
        pe_gate = sem("pe_gate")
        v_gate = sem("v_gate")
        v_lead = sem("v_lead")
        act_share = sem("act_share")
        v_comb = sem("v_comb")
        v_xhi = sem("v_xhi")
        v_xlo = sem("v_xlo")
        pe_hid = sem("pe_hid")
        act_h = sem("act_h")
        v_hhi = sem("v_hhi")
        v_hlo = sem("v_hlo")
        pe_y = sem("f_pe_y")
        v_y = sem("v_y")
        stored = sem("stored")

        STEPS = EXPERTS * KH
        LAG = 2
        CHAIN = 7

        x_view = x_in.rearrange("(g j p) d -> g p j d", j=TILES, p=P)
        out_view = out.rearrange("(g j p) d -> g p j d", j=TILES, p=P)

        def pipeline(eng, prepare, main):
            for piece in range(4):
                prepare(0, piece)
            main(0, lambda piece: prepare(1, piece))
            with eng.Fori(1, BLOCKS - 1) as g:
                main(g, lambda piece: prepare(g + 1, piece))
            main(BLOCKS - 1, lambda piece: None)

        AT = {4: 0, 10: 1, 16: 2}

        block = ctx.enter_context(nc.Block())

        @block.sync
        def _(sp):
            def load_x(g):
                sp.dma_start(y[:, g],
                             x_view[g]
                             ).then_inc(x_loaded, 16)

            load_x(0)
            for dst, src in ((wg[:], t["wg"].rearrange("(k p) e -> p k e", p=P)), (ident[:], t["ident"]),
                             (iota[:], t["iota"])):
                sp.dma_start(dst, src).then_inc(w_loaded, 16)
            for e in range(EXPERTS):
                if e:
                    sp.wait_ge(v_w1, e)
                sp.dma_start(w1_raw[:], t["w1"][e].rearrange("(k p) n -> p k n", p=P)).then_inc(w1_in, 16)
                if e:
                    sp.wait_ge(v_w2, e)
                sp.dma_start(w2_raw[:], t["w2"][e].rearrange("(k p) n -> p k n", p=P)).then_inc(w2_in, 16)
                if 0 < e < BLOCKS:
                    sp.wait_ge(x_loaded, 16 * e)
                    load_x(e)

            def store(g):
                sp.wait_ge(v_y, (g + 1) * EXPERTS * TILES)
                sp.dma_start(out_view[g],
                             y[:, g]).then_inc(stored, 16)

            with sp.Fori(0, BLOCKS) as g:
                store(g)
            sp.wait_ge(stored, 16 * BLOCKS)

        @block.tensor
        def _(pe):
            pe.wait_ge(w_loaded, 16 * 3)

            def prepare(g, piece):
                if piece == 1:
                    pe.wait_ge(v_norm, g + 1)
                    for j in range(TILES):
                        n = g * TILES + j
                        if j:
                            pe.wait_ge(act_nt, n)
                        elif not (type(g) is int and g == 0):
                            pe.wait_ge(v_gate, g)
                        for k in range(KD):
                            last = pe.transpose(psum[:, MISC, k * P:(k + 1) * P],
                                                normed[:, j, k * P:(k + 1) * P], ident[:])
                        last.then_inc(pe_nt, 1)
                if piece == 2:
                    pe.wait_ge(act_nt, (g + 1) * TILES)
                    for j in range(TILES):
                        for k in range(KD):
                            last = pe.matmul(psum[:, MISC, j * EXPERTS:(j + 1) * EXPERTS],
                                             n_t[:, k, j * P:(j + 1) * P], wg[:, k, :], start=k == 0,
                                             stop=k == KD - 1)
                    last.then_inc(pe_gate, 1)

            def hidden(g, s):
                e, m = s // KH, s % KH
                n = g * STEPS + s
                if s == 0:
                    pe.wait_ge(v_xlo, g + 1)
                if m == 0 and type(g) is int and g == 0:
                    pe.wait_ge(v_w1, e + 1)
                if not (type(g) is int and g == 0 and s < 2):
                    pe.wait_ge(act_h, n - 1)
                cols = slice(m * P, (m + 1) * P)
                for d in range(KD):
                    for a, b in ((w1_hi, x_hi), (w1_lo, x_hi), (w1_hi, x_lo)):
                        for half in range(2):
                            last = pe.matmul(psum[:, HID + 2 * (s % 2) + half, 0:HALF], a[:, e, d, cols],
                                             b[:, d, half * HALF:(half + 1) * HALF], start=d == 0 and a is w1_hi
                                             and b is x_hi, stop=d == KD - 1 and b is x_lo)
                last.then_inc(pe_hid, 1)

            def outputs(g, s):
                e, m = s // KH, s % KH
                n = g * STEPS + s
                if m == 0 and type(g) is int and g == 0:
                    pe.wait_ge(v_w2, e + 1)
                pe.wait_ge(v_hlo, n + 1)
                for j in range(TILES):
                    if m == 0 and j % 2 == 0 and not (type(g) is int and g == 0 and e == 0):
                        pe.wait_ge(v_y, (g * EXPERTS + e - 1) * TILES + min(j + 2, TILES))
                    rows = slice(j * P, (j + 1) * P)
                    dst = psum[:, Y + j // 2, (j % 2) * D:(j % 2 + 1) * D]
                    pe.matmul(dst, h_hi[s % 2][:, rows], w2_hi[:, e, m, :], start=m == 0 and j % 2 == 0, stop=False,
                              skip_group_check=True)
                    pe.matmul(dst, h_lo[s % 2][:, rows], w2_hi[:, e, m, :], start=False, stop=False,
                              skip_group_check=True)
                    last = pe.matmul(dst, h_hi[s % 2][:, rows], w2_lo[:, e, m, :], start=False, stop=m == KH - 1,
                                     skip_group_check=True)
                last.then_inc(pe_y, 1)

            def main(g, more):
                for s in range(STEPS):
                    hidden(g, s)
                    if s >= LAG:
                        outputs(g, s - LAG)
                    if s in AT:
                        more(AT[s])
                for s in range(STEPS - LAG, STEPS):
                    outputs(g, s)

            pipeline(pe, prepare, main)

        @block.scalar
        def _(act):
            def prepare(g, piece):
                if piece == 1:
                    for j in range(TILES):
                        act.wait_ge(pe_nt, g * TILES + j + 1)
                        act.copy(n_t[:, :, j * P:(j + 1) * P], psum[:, MISC, 0:KD * P].rearrange(
                            "p (k l) -> p k l", k=KD)).then_inc(act_nt, 1)
                if piece == 2:
                    act.wait_ge(v_lead, g + 1)
                    act.activation(share[:], lead[:], ACT.Tanh, scale=0.5).then_inc(act_share, 1)

            def main(g, more):
                for s in range(STEPS):
                    n = g * STEPS + s
                    act.wait_ge(pe_hid, n + 1)
                    if not (type(g) is int and g == 0 and s < 2):
                        act.wait_ge(v_hlo, n - 1)
                    act.activation(h[s % 2][:].rearrange("p (a b) -> p a b", a=2),
                                   psum[:, HID + 2 * (s % 2):HID + 2 * (s % 2) + 2, 0:HALF], ACT.Silu
                                   ).then_inc(act_h, 1)
                    if s in AT:
                        more(AT[s])

            pipeline(act, prepare, main)

        @block.gpsimd
        def _(pool):
            pool.wait_ge(prep, 1)

            def prepare(g, piece):
                if piece == 0:
                    pool.wait_ge(v_var, g + 1)
                    pool.tensor_tensor(rstd[:], var_eps[:], neg_half[:], ALU.pow).then_inc(p_rstd, 1)

            def main(g, more):
                more(0)

            pipeline(pool, prepare, main)

        @block.vector
        def _(dve):
            dve.memset(neg_half[:], -0.5).then_inc(prep, 1)
            dve.wait_ge(w_loaded, 16 * 3)

            def split_weights(e):
                dve.wait_ge(w1_in, 16 * (e + 1))
                dve.tensor_copy(w1_hi[:, e], w1_raw[:]).then_inc(v_w1hi, 1)
                dve.wait_ge(v_w1hi, e + 1)
                dve.tensor_tensor(w1_lo[:, e], w1_raw[:], w1_hi[:, e].bitcast(F32), ALU.subtract).then_inc(v_w1, 1)
                dve.wait_ge(w2_in, 16 * (e + 1))
                dve.tensor_copy(w2_hi[:, e], w2_raw[:]).then_inc(v_w2hi, 1)
                dve.wait_ge(v_w2hi, e + 1)
                dve.tensor_tensor(w2_lo[:, e], w2_raw[:], w2_hi[:, e].bitcast(F32), ALU.subtract).then_inc(v_w2, 1)

            def routing(g):
                step = [0]

                def then(ins):
                    step[0] += 1
                    if step[0] == 1:
                        ins.then_inc(v_gate, 1)
                        waits = [(v_gate, g + 1)]
                    else:
                        ins.then_inc(v_comb, 1)
                        waits = [(v_comb, g * CHAIN + step[0] - 1)]
                    if step[0] < 3:
                        wait_before(dve, idle[:, step[0]:step[0] + 1], waits)
                    else:
                        dve.wait_ge(*waits[0])

                tiles = slice(0, TILES)
                dve.wait_ge(pe_gate, g + 1)
                then(dve.tensor_copy(gates[:], psum[:, MISC, 0:TILES * EXPERTS].rearrange("p (j e) -> p j e", j=TILES)))
                for j in range(TILES):
                    last = dve.max(best[:, j, :], gates[:, j, :])
                then(last)
                for j in range(TILES):
                    last = dve.max_index(best_at[:, j, :], best[:, j, :], gates[:, j, :])
                then(last)
                then(dve.tensor_copy(best_f[:], best_at[:]))
                dve.tensor_tensor(lead[:, 0, tiles], best[:, :, 0], best[:, :, 1], ALU.subtract)
                dve.tensor_tensor(lead[:, 1, tiles], best[:, :, 1], best[:, :, 0], ALU.subtract).then_inc(v_lead, 1)
                dve.tensor_tensor(is_top[:, 0], bc_mid(iota[:], TILES), bc_last(best_f[:, :, 0], EXPERTS), ALU.is_equal)
                then(dve.tensor_tensor(is_top[:, 1], bc_mid(iota[:], TILES), bc_last(best_f[:, :, 1], EXPERTS),
                                       ALU.is_equal))
                dve.wait_ge(act_share, g + 1)
                then(dve.tensor_scalar(lead[:], share[:], 0.5, 0.5, ALU.mult, ALU.add))
                dve.tensor_tensor(is_top[:, 0], is_top[:, 0], bc_last(lead[:, 0, :], EXPERTS), ALU.mult)
                then(dve.tensor_tensor(is_top[:, 1], is_top[:, 1], bc_last(lead[:, 1, :], EXPERTS), ALU.mult))
                then(dve.tensor_tensor(combine[:, g], is_top[:, 0], is_top[:, 1], ALU.add))
                assert step[0] == CHAIN + 1

            def prepare(g, piece):
                if piece == 0:
                    dve.wait_ge(x_loaded, 16 * (g + 1))
                    for j in range(TILES):
                        last = dve.bn_stats(stats[:, j, :], y[:, g, j, :])
                    last.then_inc(v_ln, 1)
                    wait_before(dve, idle[:, 0:1], [(v_ln, 2 * g + 1)])
                    for j in range(TILES):
                        last = dve.bn_aggr(mean_var[:, j, :], stats[:, j, :])
                    last.then_inc(v_ln, 1)
                    dve.wait_ge(v_ln, 2 * g + 2)
                    dve.tensor_scalar(var_eps[:], mean_var[:, :, 1], EPS, None, ALU.add).then_inc(v_var, 1)
                if piece == 1:
                    dve.wait_ge(p_rstd, g + 1)
                    for j in range(TILES):
                        last = dve.tensor_scalar(normed[:, j, :], y[:, g, j, :], mean_var[:, j, 0:1],
                                                 rstd[:, j:j + 1], ALU.subtract, ALU.mult)
                    last.then_inc(v_norm, 1)
                if piece == 2:
                    routing(g)
                if piece == 3:
                    dve.wait_ge(act_nt, (g + 1) * TILES)
                    if not (type(g) is int and g == 0):
                        dve.wait_ge(pe_hid, g * STEPS)
                    dve.tensor_copy(x_hi[:], n_t[:]).then_inc(v_xhi, 1)
                    dve.wait_ge(v_xhi, g + 1)
                    dve.tensor_tensor(x_lo[:], n_t[:], x_hi[:].bitcast(F32), ALU.subtract).then_inc(v_xlo, 1)

            def add_outputs(g, e):
                dve.wait_ge(pe_y, g * STEPS + (e + 1) * KH)
                for j in range(TILES):
                    dve.scalar_tensor_tensor(y[:, g, j, :], psum[:, Y + j // 2, (j % 2) * D:(j % 2 + 1) * D],
                                             combine[:, g, j, e:e + 1], y[:, g, j, :], ALU.mult, ALU.add).then_inc(v_y, 1)

            def main(g, more):
                first = type(g) is int and g == 0
                if first:
                    split_weights(0)
                for s in range(STEPS):
                    n = g * STEPS + s
                    if s % KH == 1 and s > KH:
                        add_outputs(g, s // KH - 1)
                    dve.wait_ge(act_h, n + 1)
                    if not (first and s < 2):
                        dve.wait_ge(pe_y, n - 1)
                    dve.tensor_copy(h_hi[s % 2][:], h[s % 2][:]).then_inc(v_hhi, 1)
                    dve.wait_ge(v_hhi, n + 1)
                    dve.tensor_tensor(h_lo[s % 2][:], h[s % 2][:], h_hi[s % 2][:].bitcast(F32), ALU.subtract
                                      ).then_inc(v_hlo, 1)
                    if first and s % KH == 0 and s // KH + 1 < EXPERTS:
                        split_weights(s // KH + 1)
                    if s in AT:
                        more(AT[s])
                more(3)
                add_outputs(g, EXPERTS - 1)

            pipeline(dve, prepare, main)


def build_decoder(nc, t, out):
    x2 = nc.dram_tensor("x2_scratch", (SEQS, L, D), F32).ap()
    with nc.sbuf_tensor("x_res", [L, SEQS, D], F32) as x_res:
        mamba_block(nc, x_res, t)
        cross_block(nc, x_res, x2, t)
    moe_block(nc, x2.rearrange("s l d -> (s l) d"), out.rearrange("s l d -> (s l) d"), t)


def constants():
    eye = np.eye(P, dtype=np.float32)
    square = np.ones((L, L), np.float32)
    row, head = np.arange(P)[:, None], np.arange(NH)[:, None]
    group = np.arange(HG)[None]
    return {
        "ident": eye,
        "ones": np.ones((P, 1), np.float32),
        "upto": np.triu(square),
        "after": np.tril(square, -1),
        "block8": (row // DK == np.arange(8)[None]).astype(np.float32),
        "pick": (head // HG == group).astype(np.float32),
        "place": -(head % HG == group).astype(np.float32),
        "shift": np.concatenate([np.zeros((NH, HG * L), np.float32), np.tile(eye[:L, :L], (1, HG))]),
        "iota": np.tile(np.arange(EXPERTS, dtype=np.float32), (P, 1)),
    }


def kernel(**inputs):
    import concourse.bacc as bacc
    from concourse.bass_utils import run_bass_kernel_spmd

    a = {name: np.asarray(value) for name, value in inputs.items()}

    def columns(v):
        return v.reshape(-1, P).T

    def heads(w):
        return w.transpose(1, 0, 2).reshape(D, NH * DK)

    laid = {
        "x": a["x"],
        "w_in": a["L0_attn_in_proj_w"].T,
        "w_out": a["L0_attn_out_proj_w"].T,
        "ln_w": columns(a["L0_attn_ln_w"]),
        "ln_b": columns(a["L0_attn_ln_b"]),
        "conv_w": a["L0_attn_conv_w"],
        "conv_b": columns(a["L0_attn_conv_b"]),
        "gamma": columns(a["L0_attn_gamma"]),
        "a_log": a["L0_attn_A_log"],
        "dt_bias": a["L0_attn_dt_bias"],
        "d_even": a["L0_attn_D"][0::2],
        "d_odd": a["L0_attn_D"][1::2],
        "ctx_t": a["ctx_1024"].transpose(0, 2, 1),
        "mask": a["mask_SxS2_ik0"],
        "wq": heads(a["L0_xattn_Wq"]),
        "wk": heads(a["L0_xattn_Wk"]),
        "wv": heads(a["L0_xattn_Wv"]),
        "wo": a["L0_xattn_Wo"].T,
        "wg": a["L0_ffn_Wg"],
        "w1": a["L0_ffn_W1"],
        "w2": a["L0_ffn_W2"],
        **constants(),
    }
    nc = bacc.Bacc("TRN2", target_bir_lowering=False, num_devices=1)
    arrays, t = {}, {}
    for name, value in laid.items():
        value = np.ascontiguousarray(value)
        arrays[f"in_{name}"] = value
        t[name] = nc.dram_tensor(f"in_{name}", value.shape, mybir.dt.from_np(value.dtype), kind="ExternalInput").ap()
    out = nc.dram_tensor("out", (SEQS, L, D), F32, kind="ExternalOutput").ap()
    build_decoder(nc, t, out)
    r = run_bass_kernel_spmd(nc, [arrays], core_ids=[0])
    return r.results[0]["out"]
```

```python
from contextlib import ExitStack

import numpy as np
import concourse.bass as bass
from concourse import mybir

F32 = mybir.dt.float32
F32R = mybir.dt.float32r
I32 = mybir.dt.int32
ACT = mybir.ActivationFunctionType
ALU = mybir.AluOpType
AX = mybir.AxisListType

P = 128
SEQS, L, D = 32, 100, 256
KD = D // P
EPS = 1e-5

INNER, STATE, HEADS, HEADDIM, TAPS = 512, 128, 8, 64, 4
CONV = INNER + 2 * STATE
KX, KC = INNER // P, CONV // P
GROUP = 4
GROUPS = SEQS // GROUP
GL = GROUP * L
PRODUCT = [("dt", 0), ("conv", KX), ("gate", 0), ("conv", KX + 1), ("conv", 0), ("gate", 1), ("conv", 1),
           ("conv", 2), ("conv", 3), ("gate", 2), ("gate", 3)]
PRODUCTS = len(PRODUCT)
PARTS = [[0, 1, 2], [3, 4, 5], [6, 7, 8], [9, 10]]
LOG_TERMS = 6


def nth(kind, k):
    return sum(other == kind for other, _ in PRODUCT[:k])


def wait_before(eng, cell, waits):
    for s, v in waits:
        eng.wait_ge(s, v)
    eng.memset(cell, 0.0)


def bc_last(ap, n):
    return ap.unsqueeze(2).to_broadcast([ap.shape[0], ap.shape[1], n])


def bc_mid(ap, n):
    return ap.unsqueeze(1).to_broadcast([ap.shape[0], n, ap.shape[1]])


def mamba_block(nc, x_res, t, later):
    with ExitStack() as ctx:
        def sb(name, shape, dt=F32):
            return ctx.enter_context(nc.sbuf_tensor(name, shape, dt))

        def sem(name):
            return ctx.enter_context(nc.semaphore(name))

        w_in = sb("w_in", [P, KD, 2 * INNER + 2 * STATE + HEADS])
        w_out = sb("w_out", [P, KX, D])
        ln_w = sb("ln_w", [P, KD])
        ln_b = sb("ln_b", [P, KD])
        conv_w = sb("conv_w", [P, KC, TAPS])
        conv_b = sb("conv_b", [P, KC])
        gamma = sb("gamma", [P, KX])
        d_skip = sb("d_skip", [P, KX])
        a_neg = sb("a_neg", [L, HEADS])
        dt_bias = sb("dt_bias", [L, HEADS])
        ident = sb("ident_m", [P, P])
        upto = sb("upto", [L, L])
        after = sb("after", [L, L])
        ones = sb("ones_m", [P, 1])
        neg_half = sb("neg_half", [L, 2 * GROUP])

        stats = sb("stats", [L, GROUP, 6])
        mean_var = sb("mean_var", [L, GROUP, 2])
        var_eps = sb("var_eps", [L, 2, GROUP])
        rstd = sb("rstd", [L, 2, GROUP])
        res_scale = sb("res_scale", [L, GROUP])
        res_shift = sb("res_shift", [L, GROUP])
        normed = sb("normed", [L, GROUP, D])
        u_t = sb("u_t", [P, KD, GL])
        acc = sb("acc", [P, 2, GL])
        tanh = sb("tanh", [P, 2, GL])
        tanh_z = sb("tanh_z", [P, 2, GL])
        xbc = [sb(f"xbc{i}", [P, KC, GL]) for i in range(2)]
        gate = [sb(f"gate{i}", [P, KX, GL]) for i in range(2)]
        skip = [sb(f"skip{i}", [P, KX, GL]) for i in range(2)]
        dt_raw = sb("dt_raw", [L, GROUP, HEADS])
        dt_e = sb("dt_e", [L, GROUP, HEADS])
        dt_z = sb("dt_z", [L, GROUP, HEADS])
        dt_z2 = sb("dt_z2", [L, GROUP, HEADS])
        dt_p = sb("dt_p", [L, GROUP, HEADS])
        dt_8 = [sb(f"dt_8{i}", [L, GROUP, HEADS]) for i in range(2)]
        dt_a = [sb(f"dt_a{i}", [L, GROUP, HEADS]) for i in range(2)]

        steps = [sb(f"steps{i}", [L, HEADS, L]) for i in range(2)]
        decay = [sb(f"decay{i}", [L, HEADS, L]) for i in range(2)]
        cb = [sb(f"cb{i}", [L, L]) for i in range(2)]
        mix = [sb(f"mix{i}", [L, HEADS, L]) for i in range(2)]
        x_dt = [sb(f"x_dt{i}", [L, HEADS, HEADDIM]) for i in range(2)]
        y_skip = [sb(f"y_skip{i}", [P, KX, L]) for i in range(2)]
        gated = [sb(f"gated{i}", [P, KX, L]) for i in range(2)]
        squares = sb("squares", [P, KX, L])
        sq_half = sb("sq_half", [P, KX // 2, L])
        sq_sum = sb("sq_sum", [P, L])
        idle = sb("idle_m", [L, 1])
        ms = sb("ms", [L, 1])
        rms = sb("rms", [L, 1])

        psum = ctx.enter_context(nc.psum_tensor("psum_m", [P, 8, 512], F32))
        PROJ, CB, DECAY, XT, Y, OUT = 0, 2, 3, 5, 6, 7

        first_loaded = sem("first_loaded")
        w_loaded = sem("w_loaded")
        x_loaded = sem("x_loaded")
        prep = sem("prep")
        a_ready = sem("a_ready")
        a_done = sem("a_done")
        v_stats = sem("v_stats")
        v_aggr = sem("v_aggr")
        v_var = sem("v_var")
        p_rstd = sem("p_rstd")
        v_res = sem("v_res")
        v_norm = sem("v_norm")
        pe_norm_t = sem("pe_norm_t")
        act_u = sem("act_u")
        pe_proj = sem("pe_proj")
        proj_used = sem("proj_used")
        act_tap = sem("act_tap")
        v_tap = sem("v_tap")
        act_tanh = sem("act_tanh")
        v_xbc = sem("v_xbc")
        act_zt = sem("act_zt")
        v_chain = sem("v_chain")
        act_dt = sem("act_dt")
        v_dt = sem("v_dt")
        p_skip = sem("p_skip")
        p_steps = sem("p_steps")
        pe_decay = sem("pe_decay")
        act_decay = sem("act_decay")
        pe_cb = sem("pe_cb")
        v_cb = sem("v_cb")
        pe_xt = sem("pe_xt")
        v_xdt = sem("v_xdt")
        p_mix = sem("p_mix")
        pe_y = sem("pe_y")
        v_yskip = sem("v_yskip")
        v_gated = sem("v_gated")
        act_sq = sem("act_sq")
        p_half = sem("p_half")
        p_sum = sem("p_sum")
        pe_out = sem("pe_out")
        v_ms = sem("v_ms")
        p_rms = sem("p_rms")
        v_x1 = sem("v_x1")

        FIRST, WEIGHTS = 3, 12
        x_view = t["x"].rearrange("s l d -> l s d")
        PREP = 2 + KX + 1
        CHAIN = 7 + LOG_TERMS

        def proj(k):
            return psum[:, PROJ + k % 2, 0:GL]

        def by_seq(ap):
            return ap.rearrange("p (b l) -> p b l", b=GROUP)

        def with_part(a_part, *hooks):
            if a_part:
                a_part(*hooks)
            else:
                for hook in hooks:
                    hook()

        def call_hooks(hooks, part, k):
            if k == PARTS[part][-1]:
                for hook in hooks:
                    hook()

        def pipeline(eng, head, set_up, stage_a, stage_b, tail):
            head(0)
            set_up()
            for part in range(GROUP):
                stage_a(0, 0, part)
            def pair(g0, last):
                for i in range(2):
                    for q in range(GROUP):
                        more = not (last and i == 1)
                        stage_b(g0 + i, i, q, (lambda *hooks: stage_a(g0 + i + 1, 1 - i, q, hooks)) if more else None, not more and q == GROUP - 1)
            pair(0, False)
            with eng.Fori(1, GROUPS // 2 - 1) as m:
                pair(2 * m, False)
            pair(GROUPS - 2, True)
            tail()

        block = ctx.enter_context(nc.Block())

        @block.sync
        def _(sp):
            sp.dma_start(x_res[:, 0:GROUP, :], x_view[:, 0:GROUP, :]).then_inc(x_loaded, 16)
            for dst, src in ((ident[:], t["ident"]), (ln_w[:], t["ln_w"]), (ln_b[:], t["ln_b"])):
                sp.dma_start(dst, src).then_inc(first_loaded, 16)
            loads = [
                (w_in[:], t["w_in"].rearrange("(k p) n -> p k n", p=P)),
                (w_out[:], t["w_out"].rearrange("(k p) n -> p k n", p=P)),
                (conv_w[:], t["conv_w"].rearrange("(i p) k -> p i k", p=P)),
                (conv_b[:], t["conv_b"]), (gamma[:], t["gamma"]),
                (a_neg[:], t["a_log"].partition_broadcast(L)),
                (dt_bias[:], t["dt_bias"].partition_broadcast(L)),
                (upto[:], t["upto"]), (after[:], t["after"]),
            ]
            for dst, src in loads:
                sp.dma_start(dst, src).then_inc(w_loaded, 16)
            sp.dma_start(d_skip[0:HEADDIM, :], t["d_even"].partition_broadcast(HEADDIM)).then_inc(w_loaded, 16)
            sp.dma_start(d_skip[HEADDIM:P, :], t["d_odd"].partition_broadcast(HEADDIM)).then_inc(w_loaded, 16)
            sp.dma_start(ones[:], t["ones"]).then_inc(w_loaded, 16)
            for g in range(1, GROUPS):
                sp.wait_ge(x_loaded, 16 * g)
                sp.dma_start(x_res[:, g * GROUP:(g + 1) * GROUP, :],
                             x_view[:, g * GROUP:(g + 1) * GROUP, :]).then_inc(x_loaded, 16)
            later.load(sp)

        @block.tensor
        def _(pe):
            pe.wait_ge(first_loaded, 16 * FIRST)

            def head_half(g, k):
                if not (type(g) is int and g == 0):
                    pe.wait_ge(proj_used, g * PRODUCTS - 1 + k)
                pe.wait_ge(v_norm, g + 1)
                for b in range(GROUP):
                    last = pe.transpose(psum[:, PROJ + 1 - k, b * L:(b + 1) * L],
                                        normed[:, b, k * P:(k + 1) * P], ident[0:L, 0:L])
                last.then_inc(pe_norm_t, 1)

            def stage_a_head(g):
                for k in range(KD):
                    head_half(g, k)

            def stage_a(g, i, part, hooks=()):
                if part == 0:
                    pe.wait_ge(act_u, g + 1)
                for k in PARTS[part]:
                    kind, tile = PRODUCT[k]
                    call_hooks(hooks, part, k)
                    if k >= 2:
                        pe.wait_ge(proj_used, g * PRODUCTS + k - 1)
                    if kind == "dt":
                        for b in range(GROUP):
                            for d in range(KD):
                                last = pe.matmul(psum[0:L, PROJ + k % 2, b * HEADS:(b + 1) * HEADS],
                                                 u_t[:, d, b * L:(b + 1) * L], w_in[:, d, 2 * INNER + 2 * STATE:],
                                                 start=d == 0, stop=d == KD - 1)
                    else:
                        cols = (tile if kind == "gate" else KX + tile) * P
                        for d in range(KD):
                            last = pe.matmul(proj(k), w_in[:, d, cols:cols + P], u_t[:, d, :],
                                             start=d == 0, stop=d == KD - 1)
                    last.then_inc(pe_proj, 1)

            def out(n, j):
                pe.wait_ge(p_sum, n + 1)
                if type(n) is int and n == 0:
                    pe.wait_ge(prep, PREP)
                else:
                    pe.wait_ge(v_x1, n)
                pe.matmul(psum[0:L, OUT, D:D + 1], sq_sum[:], ones[:], start=True, stop=True)
                for c in range(KX):
                    last = pe.matmul(psum[0:L, OUT, 0:D], gated[j][:, c, :], w_out[:, c, :],
                                     start=c == 0, stop=c == KX - 1)
                last.then_inc(pe_out, 1)

            def mix_tokens(n, j):
                pe.wait_ge(p_mix, n + 1)
                pe.wait_ge(v_xdt, n + 1)
                if not (type(n) is int and n == 0):
                    pe.wait_ge(v_yskip, n)
                for h in range(HEADS):
                    half = HEADDIM * (h % 2)
                    last = pe.matmul(psum[half:half + HEADDIM, Y, (h // 2) * L:(h // 2 + 1) * L],
                                     x_dt[j][:, h, :], mix[j][:, h, :], start=True, stop=True)
                last.then_inc(pe_y, 1)

            def stage_b(g, i, q, a_part, final):
                n, j = g * GROUP + q, q % 2
                first = type(n) is int and n == 0
                seq = slice(q * L, (q + 1) * L)
                head = q == 0 and a_part
                pe.wait_ge(p_steps, n + 1)
                if not first:
                    pe.wait_ge(act_decay, n)
                for half in range(2):
                    last = pe.matmul(psum[0:L, DECAY + half, 0:GL], after[:],
                                     steps[j][:, half * 4:half * 4 + 4, :], start=True, stop=True)
                last.then_inc(pe_decay, 1)
                if head:
                    head_half(g + 1, 0)
                pe.wait_ge(v_xbc, g * KC + 2)
                if not first:
                    pe.wait_ge(v_cb, n)
                pe.matmul(psum[0:L, CB, 0:L], xbc[i][:, KX, seq], xbc[i][:, KX + 1, seq],
                          start=True, stop=True).then_inc(pe_cb, 1)
                pe.wait_ge(v_xbc, (g + 1) * KC)
                if not first:
                    pe.wait_ge(v_xdt, n)
                for c in range(KX):
                    last = pe.transpose(psum[0:L, XT, c * P:(c + 1) * P], xbc[i][:, c, seq], ident[:])
                last.then_inc(pe_xt, 1)
                if head:
                    head_half(g + 1, 1)
                with_part(a_part, lambda: None if first else out(n - 1, 1 - j), lambda: mix_tokens(n, j))

            pipeline(pe, stage_a_head, lambda: pe.wait_ge(w_loaded, 16 * WEIGHTS), stage_a, stage_b, lambda: out(SEQS - 1, 1))

        @block.scalar
        def _(act):
            act.wait_ge(first_loaded, 16 * FIRST)

            def set_up():
                act.wait_ge(w_loaded, 16 * WEIGHTS)
                act.activation(a_neg[:], a_neg[:], ACT.Exp).then_inc(a_ready, 1)

            def stage_a_head(g):
                for k in range(KD):
                    act.wait_ge(pe_norm_t, KD * g + k + 1)
                    last = act.activation(u_t[:, k, :], psum[:, PROJ + 1 - k, 0:GL], ACT.Identity,
                                          scale=ln_w[:, k:k + 1], bias=ln_b[:, k:k + 1])
                last.then_inc(act_u, 1)

            def conv_tanh(g, k):
                e = nth("conv", k)
                act.wait_ge(proj_used, g * PRODUCTS + k + 1)
                act.activation(tanh[:, e % 2, :], acc[:, e % 2, :], ACT.Tanh, scale=0.5).then_inc(act_tanh, 1)

            def stage_a(g, i, part, hooks=()):
                for k in PARTS[part]:
                    if k == PARTS[part][-1] and PRODUCT[k - 1][0] == "conv":
                        conv_tanh(g, k - 1)
                    call_hooks(hooks, part, k)
                    kind, c = PRODUCT[k]
                    e = nth(kind, k)
                    if kind == "dt":
                        act.wait_ge(v_chain, g * CHAIN + 1)
                        act.activation(dt_e[:], dt_z[:], ACT.Exp).then_inc(act_dt, 1)
                    if kind == "conv":
                        if not (type(g) is int and g == 0) or e >= 2:
                            act.wait_ge(v_xbc, g * KC + e - 1)
                        act.wait_ge(pe_proj, g * PRODUCTS + k + 1)
                        act.activation(acc[:, e % 2, :], proj(k), ACT.Identity, scale=conv_w[:, c, TAPS - 1:TAPS],
                                       bias=conv_b[:, c:c + 1]).then_inc(act_tap, 1)
                    if kind == "gate":
                        act.wait_ge(pe_proj, g * PRODUCTS + k + 1)
                        if e >= 2:
                            act.wait_ge(proj_used, g * PRODUCTS + PRODUCT.index(("gate", e - 2)) + 1)
                        act.activation(tanh_z[:, e % 2, :], proj(k), ACT.Tanh, scale=0.5).then_inc(act_zt, 1)
                    if k and PRODUCT[k - 1][0] == "conv" and k != PARTS[part][-1]:
                        conv_tanh(g, k - 1)

            def square(n, j):
                act.wait_ge(v_gated, n + 1)
                if not (type(n) is int and n == 0):
                    act.wait_ge(p_half, n)
                act.activation(squares[:], gated[j][:], ACT.Square).then_inc(act_sq, 1)

            def stage_b(g, i, q, a_part, final):
                n, j = g * GROUP + q, q % 2
                act.wait_ge(pe_decay, n + 1)
                if not (type(n) is int and n < 2):
                    act.wait_ge(p_mix, n - 1)
                act.activation(decay[j][:].rearrange("p (a b) l -> p a (b l)", a=2), psum[0:L, DECAY:DECAY + 2, 0:GL],
                               ACT.Exp).then_inc(act_decay, 1)
                if q == 0 and a_part:
                    stage_a_head(g + 1)
                with_part(a_part, lambda: None, lambda: square(n, j))

            pipeline(act, stage_a_head, set_up, stage_a, stage_b, lambda: None)

        @block.gpsimd
        def _(pool):
            pool.wait_ge(prep, 1)

            def make_steps(n, i, q):
                j = q % 2
                if not (type(n) is int and n < 2):
                    pool.wait_ge(pe_decay, n - 1)
                pool.tensor_tensor(steps[j][:], bc_mid(upto[:], HEADS), bc_last(dt_a[i][:, q, :], L),
                                   ALU.mult).then_inc(p_steps, 1)

            def power(g):
                pool.wait_ge(v_var, g + 1)
                pool.tensor_tensor(rstd[:], var_eps[:], neg_half[:].rearrange("p (a b) -> p a b", a=2),
                                   ALU.pow).then_inc(p_rstd, 1)

            def skips(g, i, c):
                pool.wait_ge(v_xbc, g * KC + 2 + c + 2)
                pool.tensor_tensor(skip[i][:, c:c + 2, :], xbc[i][:, c:c + 2, :], bc_last(d_skip[:, c:c + 2], GL),
                                   ALU.mult).then_inc(p_skip, 1)

            def stage_a(g, i, part, hooks=()):
                if part == 3 and type(g) is int and g == 0:
                    pool.wait_ge(v_dt, 1)
                    make_steps(0, 0, 0)
                if part == 1 and not (type(g) is int and g == GROUPS - 1):
                    power(g + 1)
                if part == 3:
                    skips(g, i, 0)

            def power_rms(n):
                pool.wait_ge(v_ms, n + 1)
                pool.tensor_tensor(rms[:], ms[:], neg_half[:, 0:1], ALU.pow).then_inc(p_rms, 1)

            def stage_b(g, i, q, a_part, final):
                n, j = g * GROUP + q, q % 2
                pool.wait_ge(act_decay, n + 1)
                pool.wait_ge(v_cb, n + 1)
                pool.tensor_tensor(mix[j][:], decay[j][:], bc_mid(cb[j][:], HEADS), ALU.mult).then_inc(p_mix, 1)
                if not final:
                    if q == GROUP - 1:
                        pool.wait_ge(v_dt, g + 2)
                        make_steps(n + 1, 1 - i, 0)
                    else:
                        make_steps(n + 1, i, q + 1)
                if a_part:
                    a_part()
                if q == 0:
                    skips(g, i, 2)
                if not (type(n) is int and n == 0):
                    power_rms(n - 1)
                sum_squares(n)

            def sum_squares(n):
                pool.wait_ge(act_sq, n + 1)
                pool.tensor_tensor(sq_half[:], squares[:, 0:2, :], squares[:, 2:4, :], ALU.add).then_inc(p_half, 1)
                pool.wait_ge(p_half, n + 1)
                if not (type(n) is int and n == 0):
                    pool.wait_ge(pe_out, n)
                pool.tensor_tensor(sq_sum[:], sq_half[:, 0, :], sq_half[:, 1, :], ALU.add).then_inc(p_sum, 1)

            pipeline(pool, power, lambda: pool.wait_ge(prep, PREP), stage_a, stage_b, lambda: power_rms(SEQS - 1))

        @block.vector
        def _(dve):
            dve.memset(neg_half[:], -0.5).then_inc(prep, 1)

            def set_up():
                dve.wait_ge(w_loaded, 16 * WEIGHTS)
                for c in range(KX):
                    dve.tensor_scalar(w_out[:, c, :], w_out[:, c, :], gamma[:, c:c + 1], None, ALU.mult
                                      ).then_inc(prep, 1)
                dve.tensor_scalar(d_skip[:], d_skip[:], 0.5, None, ALU.mult).then_inc(prep, 1)
                dve.wait_ge(a_ready, 1)
                dve.tensor_scalar(a_neg[:], a_neg[:], -1.0, None, ALU.mult).then_inc(prep, 1)
                dve.wait_ge(prep, PREP)

            def norm_statistics(g):
                dve.wait_ge(x_loaded, (g + 1) * 16)
                for b in range(GROUP):
                    last = dve.bn_stats(stats[:, b, :], x_res[:, g * GROUP + b, :])
                last.then_inc(v_stats, 1)
                wait_before(dve, idle[0:L, :], [(v_stats, g + 1)])
                for b in range(GROUP):
                    last = dve.bn_aggr(mean_var[:, b, :], stats[:, b, :])
                last.then_inc(v_aggr, 1)
                dve.wait_ge(v_aggr, g + 1)
                dve.tensor_scalar(var_eps[:, 0, :], mean_var[:, :, 1], EPS, None, ALU.add)
                dve.tensor_scalar(var_eps[:, 1, :], mean_var[:, :, 1], 1.0 + EPS, EPS * EPS, ALU.mult,
                                  ALU.add).then_inc(v_var, 1)

            def normalize(g):
                dve.wait_ge(p_rstd, g + 1)
                dve.tensor_scalar(res_scale[:], rstd[:, 0, :], 1.0, None, ALU.add)
                dve.scalar_tensor_tensor(res_shift[:], mean_var[:, :, 0], -1.0, rstd[:, 0, :], ALU.mult,
                                         ALU.mult).then_inc(v_res, 1)
                if not (type(g) is int and g == 0):
                    dve.wait_ge(pe_norm_t, KD * g)
                for b in range(GROUP):
                    last = dve.tensor_scalar(normed[:, b, :], x_res[:, g * GROUP + b, :], mean_var[:, b, 0:1],
                                             rstd[:, 1, b:b + 1], ALU.subtract, ALU.mult)
                last.then_inc(v_norm, 1)
                dve.wait_ge(v_res, g + 1)
                for b in range(GROUP):
                    dve.tensor_scalar(x_res[:, g * GROUP + b, :], x_res[:, g * GROUP + b, :], res_scale[:, b:b + 1],
                                      res_shift[:, b:b + 1], ALU.mult, ALU.add)

            def taps(g, k, e, c):
                a, src = by_seq(acc[:, e % 2, :]), by_seq(proj(k))
                dve.wait_ge(act_tap, g * KC + e + 1)
                for back in range(1, TAPS):
                    if back > 1:
                        dve.wait_ge(v_tap, (g * KC + e) * 2 + back - 1)
                    dve.scalar_tensor_tensor(a[:, :, back:], src[:, :, 0:L - back],
                                             conv_w[:, c, TAPS - 1 - back:TAPS - back], a[:, :, back:],
                                             ALU.mult, ALU.add).then_inc(v_tap if back < TAPS - 1 else proj_used, 1)

            def silu(g, i, e, c):
                dve.wait_ge(act_tanh, g * KC + e + 1)
                dve.scalar_tensor_tensor(xbc[i][:, c, :], tanh[:, e % 2, :], 1.0, acc[:, e % 2, :],
                                         ALU.add, ALU.mult).then_inc(v_xbc, 1)

            def dt_start(g):
                dve.wait_ge(pe_proj, g * PRODUCTS + 1)
                dve.tensor_tensor(dt_raw[:], psum[0:L, PROJ, 0:GROUP * HEADS].rearrange(
                    "p (b h) -> p b h", b=GROUP), bc_mid(dt_bias[:], GROUP), ALU.add).then_inc(proj_used, 1)
                dve.wait_ge(proj_used, g * PRODUCTS + 1)
                dve.scalar_tensor_tensor(dt_z[:], dt_raw[:], -1.0, dt_raw[:], ALU.mult, ALU.min).then_inc(v_chain, 1)

            def then(g, step, ins):
                ins.then_inc(v_chain, 1)
                dve.wait_ge(v_chain, g * CHAIN + step)

            def softplus_argument(g):
                dve.tensor_scalar(dt_raw[:], dt_raw[:], 0.0, None, ALU.max)
                dve.wait_ge(act_dt, g + 1)
                then(g, 2, dve.tensor_scalar(dt_p[:], dt_e[:], 2.0, None, ALU.add))
                then(g, 3, dve.reciprocal(dt_p[:], dt_p[:]))
                then(g, 4, dve.tensor_tensor(dt_z[:], dt_e[:], dt_p[:], ALU.mult))
                then(g, 5, dve.tensor_tensor(dt_z2[:], dt_z[:], dt_z[:], ALU.mult))
                then(g, 6, dve.tensor_scalar(dt_p[:], dt_z2[:], 1.0 / (2 * LOG_TERMS + 1), None, ALU.mult))

            def softplus_series(g, i):
                for m in range(LOG_TERMS - 1, 0, -1):
                    then(g, 6 + LOG_TERMS - m, dve.scalar_tensor_tensor(
                        dt_p[:], dt_p[:], 1.0 / (2 * m + 1), dt_z2[:], ALU.add, ALU.mult))
                last = 5 + LOG_TERMS
                then(g, last + 1, dve.scalar_tensor_tensor(dt_p[:], dt_p[:], 1.0, dt_z[:], ALU.add, ALU.mult))
                then(g, last + 2, dve.scalar_tensor_tensor(dt_raw[:], dt_p[:], 2.0, dt_raw[:], ALU.mult, ALU.add))
                dve.tensor_scalar(dt_8[i][:], dt_raw[:], 0.125, None, ALU.mult)
                dve.tensor_tensor(dt_a[i][:], dt_raw[:], bc_mid(a_neg[:], GROUP), ALU.mult).then_inc(v_dt, 1)
                assert last + 2 == CHAIN

            def stage_a(g, i, part, hooks=()):
                more = not (type(g) is int and g == GROUPS - 1)
                if part == 0 and more:
                    norm_statistics(g + 1)
                if part == 1:
                    softplus_argument(g)
                if part == 2:
                    softplus_series(g, i)
                if part == 3 and more:
                    normalize(g + 1)
                for k in PARTS[part]:
                    kind, c = PRODUCT[k]
                    e = nth(kind, k)
                    call_hooks(hooks, part, k)
                    last = k == PARTS[part][-1]
                    silu_due = k and PRODUCT[k - 1][0] == "conv"
                    if silu_due and last:
                        silu(g, i, nth("conv", k - 1), PRODUCT[k - 1][1])
                    if kind == "dt":
                        dt_start(g)
                    if kind == "conv":
                        taps(g, k, e, c)
                    if kind == "gate":
                        dve.wait_ge(act_zt, g * KX + e + 1)
                        dve.scalar_tensor_tensor(gate[i][:, c, :], tanh_z[:, e % 2, :], 1.0, proj(k),
                                                 ALU.add, ALU.mult).then_inc(proj_used, 1)
                    if silu_due and not last:
                        silu(g, i, nth("conv", k - 1), PRODUCT[k - 1][1])

            def stage_a_head(g):
                norm_statistics(g)
                normalize(g)

            def residual(n):
                dve.wait_ge(p_rms, n + 1)
                dve.scalar_tensor_tensor(x_res[:, n, :], psum[0:L, OUT, 0:D], rms[:, 0:1], x_res[:, n, :],
                                         ALU.mult, ALU.add).then_inc(v_x1, 1)

            def mean_square(n):
                dve.wait_ge(pe_out, n + 1)
                dve.tensor_scalar(ms[:], psum[0:L, OUT, D:D + 1], 1.0 / INNER, 4 * EPS, ALU.mult,
                                  ALU.add).then_inc(v_ms, 1)

            def gate_tokens(n, g, i, q):
                j, seq = q % 2, slice(q * L, (q + 1) * L)
                dve.wait_ge(pe_y, n + 1)
                dve.wait_ge(p_skip, 2 * (g + 1))
                dve.tensor_tensor(y_skip[j][:], psum[:, Y, 0:GL].rearrange("p (c l) -> p c l", c=KX),
                                  skip[i][:, :, seq], ALU.add).then_inc(v_yskip, 1)
                dve.wait_ge(v_yskip, n + 1)
                dve.tensor_tensor(gated[j][:], y_skip[j][:], gate[i][:, :, seq], ALU.mult).then_inc(v_gated, 1)
                if not (type(n) is int and n == 0):
                    residual(n - 1)

            def stage_b(g, i, q, a_part, final):
                n, j = g * GROUP + q, q % 2
                first = type(n) is int and n == 0
                dve.wait_ge(pe_cb, n + 1)
                dve.tensor_tensor(cb[j][:], psum[0:L, CB, 0:L], upto[:], ALU.mult).then_inc(v_cb, 1)
                dve.wait_ge(pe_xt, n + 1)
                dve.tensor_tensor(x_dt[j][:], psum[0:L, XT, :].rearrange("p (h c) -> p h c", h=HEADS),
                                  bc_last(dt_8[i][:, q, :], HEADDIM), ALU.mult).then_inc(v_xdt, 1)
                with_part(a_part, lambda: None if first else mean_square(n - 1), lambda: gate_tokens(n, g, i, q))
                if type(n) is int and n >= SEQS - later.PIECES:
                    later.prepare(dve, n - (SEQS - later.PIECES))

            def tail():
                mean_square(SEQS - 1)
                residual(SEQS - 1)

            pipeline(dve, stage_a_head, set_up, stage_a, stage_b, tail)


C = 361
CP = C + 1
NH, DK = 16, 16
ROWS = [(0, 121), (121, 121), (242, 119)]
HG = 4
NG = NH // HG
VW = 32
MASKED = -1e30


class CrossConstants:

    LOADS = 12
    PIECES = 8

    def __init__(self, nc, ctx, t):
        def sb(name, shape, dt=F32):
            return ctx.enter_context(nc.sbuf_tensor(name, shape, dt))

        def pair(name, shape, dt=F32):
            return [sb(f"{name}{i}", shape, dt) for i in range(2)]

        self.t = t
        self.wq = sb("wq", [P, KD, D])
        self.wo = sb("wo", [P, KD, D])
        self.w_raw = sb("w_raw", [P, 2, KD, D])
        self.w_hi = sb("w_hi", [P, 2, KD, D], F32R)
        self.w_lo = sb("w_lo", [P, 2, KD, D], F32R)
        self.ident = sb("ident_c", [P, P])
        self.block4 = sb("block4", [P, HG])
        self.mask_raw = sb("mask_raw", [NH + L, C], I32)
        self.mask_row = sb("mask_row", [L, C], I32)
        self.bias_row = sb("bias_row", [L, CP])
        self.shift_w = sb("shift_w", [NH + L, NG, C], F32R)
        self.pick_raw = sb("pick_raw", [NH, NG])
        self.place = sb("place", [NH, HG])
        self.shift_raw = sb("shift_raw", [NH + L, HG * L])
        self.shift = pair("shift", [NH + L, HG * L], F32R)
        self.any_row = sb("any_row", [L, 1])
        self.any_inv = sb("any_inv", [L, 1])
        self.keep_row = sb("keep_row", [L, 1])
        self.neg_half = sb("neg_half_c", [L, 1])
        self.ctx_raw = pair("ctx_raw", [P, KD, CP])
        self.val = pair("val", [P, len(ROWS), NH, VW])

        self.loaded = ctx.enter_context(nc.semaphore("c_loaded"))
        self.ctx_in = [ctx.enter_context(nc.semaphore(f"ctx_in{i}")) for i in range(2)]
        self.ready = ctx.enter_context(nc.semaphore("c_ready"))
        self.steps = 0

    def load(self, sp):
        t = self.t
        loads = [
            (self.w_raw[:, 0], t["wk"].rearrange("(k p) n -> p k n", p=P)),
            (self.w_raw[:, 1], t["wv"].rearrange("(k p) n -> p k n", p=P)),
            (self.mask_raw[0:NH, :], t["mask"][0:NH, :]), (self.mask_raw[NH:NH + L, :], t["mask"]),
            (self.mask_row[:], t["mask"]), (self.pick_raw[:], t["pick"]), (self.place[:], t["place"]),
            (self.shift_raw[:], t["shift"]), (self.block4[:], t["block4"]), (self.ident[:], t["ident"]),
            (self.wq[:], t["wq"].rearrange("(k p) n -> p k n", p=P)),
            (self.wo[:], t["wo"].rearrange("(k p) n -> p k n", p=P)),
        ]
        assert len(loads) == self.LOADS
        for dst, src in loads:
            sp.dma_start(dst, src).then_inc(self.loaded, 16)
        for n in range(2):
            self.load_context(sp, n, n)

    def load_context(self, sp, n, p):
        sp.dma_start(self.ctx_raw[p][:, :, 0:C], self.t["ctx_t"][n].rearrange("(k q) c -> q k c", q=P)
                     ).then_inc(self.ctx_in[p], 16)

    def prepare(self, dve, piece):
        def then(ins):
            self.steps += 1
            ins.then_inc(self.ready, 1)
            dve.wait_ge(self.ready, self.steps)

        if piece == 0:
            dve.wait_ge(self.loaded, 16 * self.LOADS)
            then(dve.memset(self.neg_half[:], -0.5))
            then(dve.tensor_copy(self.w_hi[:], self.w_raw[:]))
        if piece == 1:
            then(dve.tensor_tensor(self.w_lo[:], self.w_raw[:], self.w_hi[:].bitcast(F32), ALU.subtract))
        if piece == 2:
            then(dve.memset(self.bias_row[:], MASKED))
            then(dve.tensor_scalar(self.bias_row[:, 0:C], self.mask_row[:], 0.0, MASKED, ALU.is_equal, ALU.mult))
            then(dve.tensor_reduce(self.any_row[:], self.bias_row[:], AX.X, ALU.max))
            then(dve.tensor_scalar(self.any_row[:], self.any_row[:], 0.0, None, ALU.is_equal))
            then(dve.reciprocal(self.any_inv[:], self.any_row[:]))
            then(dve.tensor_tensor(self.keep_row[:], self.any_row[:], self.any_inv[:], ALU.mult))
        if piece in (3, 4):
            for g in range(2 * (piece - 3), 2 * (piece - 2)):
                then(dve.tensor_scalar(self.shift_w[:, g, :], self.mask_raw[:], 0.0, MASKED, ALU.is_equal, ALU.mult))
                then(dve.tensor_copy(self.shift_w[0:NH, g, :], self.pick_raw[:, g:g + 1].to_broadcast([NH, C])))
        if piece == 5:
            for p in range(2):
                then(dve.memset(self.ctx_raw[p][:, :, C:CP], 0.0))
                then(dve.tensor_copy(self.shift[p][:], self.shift_raw[:]))
        if piece in (6, 7):
            then(dve.memset(self.val[piece - 6][:], 0.0))
            then(dve.memset(self.val[piece - 6][:, :, :, DK:DK + 1], 1.0))


def cross_block(nc, x_res, x_out, constants, later):
    with ExitStack() as ctx:
        def sb(name, shape, dt=F32):
            return ctx.enter_context(nc.sbuf_tensor(name, shape, dt))

        def pair(name, shape, dt=F32):
            return [sb(f"{name}{i}", shape, dt) for i in range(2)]

        def sem(name):
            return ctx.enter_context(nc.semaphore(name))

        k = constants
        wq, wo, w_hi, w_lo, ident, block4 = k.wq, k.wo, k.w_hi, k.w_lo, k.ident, k.block4
        bias_row, shift_w, place, shift, keep_row = k.bias_row, k.shift_w, k.place, k.shift, k.keep_row
        neg_half, ctx_raw, val, ctx_in = k.neg_half, k.ctx_raw, k.val, k.ctx_in

        ctx_hi = pair("ctx_hi", [P, KD, CP], F32R)
        ctx_lo = pair("ctx_lo", [P, KD, CP], F32R)
        stats = sb("stats_c", [L, 6])
        mean_var = sb("mean_var_c", [L, 2])
        var_eps = sb("var_eps_c", [L, 1])
        rstd = sb("rstd_c", [L, 1])
        normed = pair("normed_c", [L, D])
        norm_t = sb("norm_t", [P, KD, L])
        q_hi = sb("q_hi", [P, KD, 2, L], F32R)
        q_lo = sb("q_lo", [P, KD, 2, L])
        qb_hi = pair("qb_hi", [P, NG, HG * L], F32R)
        qb_lo = pair("qb_lo", [P, NG, HG * L], F32R)
        keys = pair("keys", [P, NG, CP], F32R)
        scored = pair("scored", [L, CP])
        row_max = sb("row_max", [L, NH])
        probs = pair("probs", [P, len(ROWS), 2 * HG * L])
        o_t = sb("o_t", [P, NG, L])
        rden = sb("rden", [L, NH])
        o_n = sb("o_n", [L, NH, DK])
        on_t = sb("on_t", [P, KD, L])
        x2 = pair("x2", [L, D])
        idle = sb("idle_c", [L, 1 + NH])

        psum = ctx.enter_context(nc.psum_tensor("psum_c", [P, 8, 512], F32))
        SCORE, O, KV, MISC = 0, 4, 5, 7

        x2_out = [sem(f"x2_out{i}") for i in range(2)]
        act_chi = sem("act_chi")
        p_clo = sem("p_clo")
        v_ln = sem("v_ln")
        v_var = sem("c_v_var")
        p_rstd = sem("c_p_rstd")
        v_norm = sem("c_v_norm")
        pe_nt = sem("pe_nt")
        act_nt = sem("act_nt")
        pe_q = sem("pe_q")
        act_qhi = sem("act_qhi")
        v_q = sem("v_q")
        p_qb = sem("p_qb")
        pe_k = sem("pe_k")
        act_khi = sem("act_khi")
        v_klo = sem("v_klo")
        pe_v = sem("pe_v")
        act_v = sem("act_v")
        pe_max = sem("pe_max")
        v_max = sem("v_max")
        pe_maxt = sem("pe_maxt")
        v_shift = sem("v_shift")
        pe_score = sem("pe_score")
        act_exp = sem("act_exp")
        pe_pv = sem("pe_pv")
        act_o = sem("act_o")
        pe_ot = sem("pe_ot")
        v_rden = sem("v_rden")
        v_on = sem("v_on")
        pe_ont = sem("pe_ont")
        act_ont = sem("act_ont")
        pe_wo = sem("pe_wo")
        v_x2 = sem("v_x2")

        STEPS = 2 * len(ROWS)
        NC = len(ROWS)
        HALVES = (slice(0, 64), slice(64, P))
        MIX_HALVES = (range(0, HG // 2), range(HG // 2, HG))

        def after(m, p, k):
            return m + (p + k) // 2, (p + k) % 2

        def at(m, p):
            return 2 * m + p

        def pipeline(eng, prologue, sequence):
            prologue()
            sequence(0, 0)
            sequence(0, 1)
            with eng.Fori(1, SEQS // 2 - 2) as m:
                sequence(m, 0)
                sequence(m, 1)
            for m in range(SEQS // 2 - 2, SEQS // 2):
                sequence(m, 0)
                sequence(m, 1)

        def q_psum(half):
            return psum[half, MISC, 0:KD * L].rearrange("p (k l) -> p k l", k=KD)

        max_t = psum[0:NH, SCORE, HG * L:HG * L + L]

        def has(m, p, k):
            return type(m) is not int or 0 <= 2 * m + p + k < SEQS

        block = ctx.enter_context(nc.Block())

        @block.sync
        def _(sp):
            def load(m, p):
                constants.load_context(sp, at(m, p), p)

            sp.wait_ge(act_chi, 1)
            sp.wait_ge(p_clo, 1)
            load(1, 0)

            def sequence(m, p):
                if has(m, p, 3):
                    m1, p1 = after(m, p, 1)
                    sp.wait_ge(act_chi, at(m1, p1) + 1)
                    sp.wait_ge(p_clo, at(m1, p1) + 1)
                    load(*after(m, p, 3))
                if has(m, p, -1):
                    mb, pb = after(m, p, -1)
                    sp.wait_ge(v_x2, at(mb, pb) + 1)
                    sp.dma_start(x_out[at(mb, pb)], x2[pb][:]).then_inc(x2_out[pb], 16)

                if type(m) is int and 2 * m + p == SEQS - 4:
                    for i in range(2):
                        sp.wait_ge(x2_out[i], 16 * (SEQS // 2 - 4))
                    later.load(sp)

            pipeline(sp, lambda: None, sequence)
            sp.wait_ge(v_x2, SEQS)
            sp.dma_start(x_out[SEQS - 1], x2[1][:]).then_inc(x2_out[1], 16)
            for p in range(2):
                sp.wait_ge(x2_out[p], 16 * SEQS // 2)

        @block.tensor
        def _(pe):
            pe.wait_ge(constants.ready, constants.steps)

            def split_product(out, a_hi, a_lo, b_hi, b_lo, start, stop):
                pe.matmul(out, a_hi, b_hi, start=start, stop=False)
                pe.matmul(out, a_lo, b_hi, start=False, stop=False)
                return pe.matmul(out, a_hi, b_lo, start=False, stop=stop)

            def norm_transposes(m, p):
                n = at(m, p)
                pe.wait_ge(v_norm, n + 1)
                if has(m, p, -3):
                    pe.wait_ge(v_x2, n - 2)
                elif has(m, p, -1):
                    pe.wait_ge(v_q, n)
                for k in range(KD):
                    last = pe.transpose(psum[:, MISC, k * L:(k + 1) * L], normed[p][:, k * P:(k + 1) * P],
                                        ident[0:L, 0:L])
                last.then_inc(pe_nt, 1)

            def project_q(m, p):
                pe.wait_ge(act_nt, at(m, p) + 1)
                for k in range(KD):
                    for d in range(KD):
                        last = pe.matmul(psum[:, MISC, k * L:(k + 1) * L], wq[:, d, k * P:(k + 1) * P],
                                         norm_t[:, d, :], start=d == 0, stop=d == KD - 1)
                last.then_inc(pe_q, 1)

            def project_k(m, p):
                n = at(m, p)
                pe.wait_ge(p_clo, n + 1)
                if has(m, p, -1):
                    pe.wait_ge(v_max, n * NH)
                for k in range(KD):
                    cols = slice(k * P, (k + 1) * P)
                    for d in range(KD):
                        last = split_product(psum[:, KV + k, 0:CP], w_hi[:, 0, d, cols], w_lo[:, 0, d, cols],
                                             ctx_hi[p][:, d, :], ctx_lo[p][:, d, :], d == 0, d == KD - 1)
                    last.then_inc(pe_k, 1)

            def project_v(m, p, c):
                n = at(m, p)
                if c < 2:
                    pe.wait_ge(v_klo, KD * n + c + 1)
                else:
                    pe.wait_ge(act_v, NC * n + 1)
                start, rows = ROWS[c]
                for d in range(KD):
                    last = split_product(psum[0:rows, KV + c % 2, 0:D], ctx_hi[p][:, d, start:start + rows],
                                         ctx_lo[p][:, d, start:start + rows], w_hi[:, 1, d, :], w_lo[:, 1, d, :],
                                         d == 0, d == KD - 1)
                last.then_inc(pe_v, 1)

            def max_scores(m, p, heads):
                n = at(m, p)
                for h in heads:
                    if h % 8 == 0:
                        pe.wait_ge(p_qb, 4 * n + 1 + h // 8)
                    if h == 0:
                        pe.wait_ge(v_klo, KD * (n + 1))
                    if h < 2:
                        pe.wait_ge(act_v, NC * n + 2 + h)
                    else:
                        pe.wait_ge(v_max, NH * n + h - 1)
                    g, j = h // HG, h % HG
                    pe.matmul(psum[0:L, KV + (h + 1) % 2, 0:CP], qb_hi[p][:, g, j * L:(j + 1) * L],
                              keys[p][:, g, :], start=True, stop=True).then_inc(pe_max, 1)

            def max_transpose(m, p):
                n = at(m, p)
                pe.wait_ge(v_max, NH * (n + 1))
                if has(m, p, -1):
                    pe.wait_ge(act_exp, STEPS * n)
                pe.transpose(max_t, row_max[:], ident[0:L, 0:L]).then_inc(pe_maxt, 1)

            def scores(m, p, i, halves=(0, 1)):
                n = at(m, p)
                pr, c = i // NC, i % NC
                start, rows = ROWS[c]
                if i == 0:
                    pe.wait_ge(v_shift, n + 1)
                    pe.wait_ge(p_qb, 4 * n + 4)
                if 0 in halves and not (type(m) is int and n == 0 and i < 2):
                    pe.wait_ge(act_exp, STEPS * n + i - 1)
                for half in halves:
                    g = 2 * pr + half
                    out = psum[0:rows, SCORE + 2 * (i % 2) + half, 0:HG * L]
                    cols = slice(start, start + rows)
                    pe.matmul(out, shift_w[:, g, cols], shift[p][:], start=True, stop=False)
                    pe.matmul(out, keys[p][:, g, cols], qb_hi[p][:, g, :], start=False, stop=False)
                    last = pe.matmul(out, keys[p][:, g, cols], qb_lo[p][:, g, :], start=False, stop=True)
                if 1 in halves:
                    last.then_inc(pe_score, 1)

            def mix_values(m, p, g, heads):
                n = at(m, p)
                pe.wait_ge(act_exp, STEPS * n + NC * (g // 2 + 1))
                if g == 0 and 0 in heads:
                    pe.wait_ge(act_v, NC * (n + 1))
                    if has(m, p, -1):
                        pe.wait_ge(act_o, n)
                for j in heads:
                    for c in range(NC):
                        rows = ROWS[c][1]
                        at_col = ((g % 2) * HG + j) * L
                        last = pe.matmul(psum[VW * j:VW * (j + 1), O, g * L:(g + 1) * L],
                                         val[p][0:rows, c, HG * g + j, :],
                                         probs[g // 2][0:rows, c, at_col:at_col + L], start=c == 0, stop=c == NC - 1)
                if g % 2 and HG - 1 in heads:
                    last.then_inc(pe_pv, 1)

            def o_transposes(m, p, fresh):
                n = at(m, p)
                pe.wait_ge(act_o, n + 1)
                if fresh:
                    pe.wait_ge(v_q, n + 3)
                else:
                    pe.wait_ge(v_x2, n)
                for g in range(NG):
                    last = pe.transpose(psum[0:L, MISC, g * P:(g + 1) * P], o_t[:, g, :], ident[:])
                last.then_inc(pe_ot, 1)

            def on_transposes(m, p):
                pe.wait_ge(v_on, at(m, p) + 1)
                for k in range(KD):
                    last = pe.transpose(psum[:, MISC, k * L:(k + 1) * L],
                                        o_n[:].rearrange("l h d -> l (h d)")[:, k * P:(k + 1) * P], ident[0:L, 0:L])
                last.then_inc(pe_ont, 1)

            def project_out(m, p):
                pe.wait_ge(act_ont, at(m, p) + 1)
                for k in range(KD):
                    last = pe.matmul(psum[0:L, MISC, 0:D], on_t[:, k, :], wo[:, k, :], start=k == 0, stop=k == KD - 1)
                last.then_inc(pe_wo, 1)

            def prologue():
                project_k(0, 0)
                norm_transposes(0, 0)
                project_q(0, 0)
                for c in range(NC):
                    project_v(0, 0, c)
                max_scores(0, 0, range(NH))
                max_transpose(0, 0)

            def sequence(m, p):
                nxt = after(m, p, 1) if has(m, p, 1) else None
                prv = after(m, p, -1) if has(m, p, -1) else None
                if nxt:
                    project_k(*nxt)
                    norm_transposes(*nxt)
                scores(m, p, 0)
                if nxt:
                    project_q(*nxt)
                scores(m, p, 1)
                if nxt:
                    project_v(*nxt, 0)
                    project_v(*nxt, 1)
                if prv:
                    o_transposes(*prv, bool(nxt))
                def head(h):
                    if nxt:
                        max_scores(*nxt, [h])
                scores(m, p, 2, [0])
                if nxt:
                    project_v(*nxt, 2)
                head(0)
                scores(m, p, 2, [1])
                for half in range(2):
                    head(1 + half)
                    scores(m, p, 3, [half])
                for half in range(2):
                    head(3 + half)
                    mix_values(m, p, 0, MIX_HALVES[half])
                if prv:
                    on_transposes(*prv)
                for half in range(4):
                    head(5 + half)
                    scores(m, p, 4 + half // 2, [half % 2])
                for half in range(6):
                    head(9 + half)
                    mix_values(m, p, 1 + half // 2, MIX_HALVES[half % 2])
                head(15)
                if prv:
                    project_out(*prv)
                if nxt:
                    max_transpose(*nxt)

            pipeline(pe, prologue, sequence)
            last = (SEQS // 2 - 1, 1)
            o_transposes(*last, False)
            on_transposes(*last)
            project_out(*last)

        @block.scalar
        def _(act):
            act.wait_ge(constants.ready, constants.steps)

            def split_context(m, p):
                act.wait_ge(ctx_in[p], 16 * (m + 1))
                if has(m, p, -2):
                    act.wait_ge(pe_v, NC * (at(m, p) - 1))
                act.copy(ctx_hi[p][:], ctx_raw[p][:]).then_inc(act_chi, 1)

            def norm_copy(m, p):
                act.wait_ge(pe_nt, at(m, p) + 1)
                act.copy(norm_t[:], psum[:, MISC, 0:KD * L].rearrange("p (k l) -> p k l", k=KD)).then_inc(act_nt, 1)

            def key_copy(m, p):
                for k in range(KD):
                    act.wait_ge(pe_k, KD * at(m, p) + k + 1)
                    for half in HALVES:
                        last = act.copy(keys[p][half, 2 * k + (half.start > 0), :], psum[half, KV + k, 0:CP])
                    last.then_inc(act_khi, 1)

            def queries_high(m, p):
                n = at(m, p)
                act.wait_ge(pe_q, n + 1)
                if has(m, p, -1):
                    act.wait_ge(p_qb, 4 * n)
                for half in HALVES:
                    for dst in HALVES:
                        last = act.mul(q_hi[dst, :, int(half.start > 0), :], q_psum(half), 0.25)
                last.then_inc(act_qhi, 1)

            def value_copy(m, p, c):
                act.wait_ge(pe_v, NC * at(m, p) + c + 1)
                rows = ROWS[c][1]
                act.copy(val[p][0:rows, c, :, 0:DK], psum[0:rows, KV + c % 2, 0:D].rearrange(
                    "p (h d) -> p h d", h=NH)).then_inc(act_v, 1)

            def exps(m, p, i):
                n = at(m, p)
                pr, c = i // NC, i % NC
                rows = ROWS[c][1]
                act.wait_ge(pe_score, STEPS * n + i + 1)
                if c == 0 and has(m, p, -1):
                    act.wait_ge(pe_pv, 2 * n - 1 + pr)
                act.activation(probs[pr][0:rows, c, :].rearrange("p (a b) -> p a b", a=2),
                               psum[0:rows, SCORE + 2 * (i % 2):SCORE + 2 * (i % 2) + 2, 0:HG * L],
                               ACT.Exp).then_inc(act_exp, 1)

            def o_copy(m, p):
                n = at(m, p)
                act.wait_ge(pe_pv, 2 * (n + 1))
                if has(m, p, -1):
                    act.wait_ge(pe_ot, n)
                act.copy(o_t[:], psum[:, O, 0:NG * L].rearrange("p (g l) -> p g l", g=NG)).then_inc(act_o, 1)

            def on_copy(m, p):
                n = at(m, p)
                act.wait_ge(pe_ont, n + 1)
                act.copy(on_t[:], psum[:, MISC, 0:KD * L].rearrange("p (k l) -> p k l", k=KD)).then_inc(act_ont, 1)

            def prologue():
                split_context(0, 0)
                key_copy(0, 0)
                norm_copy(0, 0)
                queries_high(0, 0)
                for c in range(NC):
                    value_copy(0, 0, c)
                split_context(0, 1)

            def sequence(m, p):
                nxt = after(m, p, 1) if has(m, p, 1) else None
                prv = after(m, p, -1) if has(m, p, -1) else None
                if nxt:
                    key_copy(*nxt)
                    norm_copy(*nxt)
                exps(m, p, 0)
                if nxt:
                    queries_high(*nxt)
                exps(m, p, 1)
                if nxt:
                    value_copy(*nxt, 0)
                    value_copy(*nxt, 1)
                if nxt:
                    value_copy(*nxt, 2)
                exps(m, p, 2)
                if has(m, p, 2):
                    split_context(*after(m, p, 2))
                exps(m, p, 3)
                if prv:
                    on_copy(*prv)
                exps(m, p, 4)
                exps(m, p, 5)
                o_copy(m, p)

            pipeline(act, prologue, sequence)
            on_copy(SEQS // 2 - 1, 1)

        @block.gpsimd
        def _(pool):
            pool.wait_ge(constants.ready, constants.steps)

            def split_context(m, p):
                n = at(m, p)
                pool.wait_ge(act_chi, n + 1)
                pool.tensor_tensor(ctx_lo[p][:], ctx_raw[p][:], ctx_hi[p][:].bitcast(F32), ALU.subtract
                                   ).then_inc(p_clo, 1)

            def block_queries(m, p):
                n = at(m, p)
                pool.wait_ge(v_q, n + 1)
                if has(m, p, -2):
                    pool.wait_ge(pe_score, STEPS * (n - 1))
                for src, dst in ((q_hi, qb_hi), (q_lo, qb_lo)):
                    for k in range(KD):
                        rows = src[:, k, :, :]
                        if src is q_hi:
                            rows = rows.bitcast(F32)
                        pool.tensor_tensor(dst[p][:, 2 * k:2 * k + 2, :].rearrange("p g (j l) -> p g j l", l=L),
                                           rows.unsqueeze(2).to_broadcast([P, 2, HG, L]),
                                           block4[:].unsqueeze(1).unsqueeze(3).to_broadcast([P, 2, HG, L]), ALU.mult
                                           ).then_inc(p_qb, 1)

            def power(m, p):
                pool.wait_ge(v_var, at(m, p) + 1)
                pool.tensor_tensor(rstd[:], var_eps[:], neg_half[:], ALU.pow).then_inc(p_rstd, 1)

            def prologue():
                split_context(0, 0)
                power(0, 0)
                power(0, 1)
                block_queries(0, 0)
                split_context(0, 1)

            def sequence(m, p):
                if has(m, p, 2):
                    power(*after(m, p, 2))
                if has(m, p, 1):
                    block_queries(*after(m, p, 1))
                if has(m, p, 2):
                    split_context(*after(m, p, 2))

                if type(m) is int and 2 * m + p == SEQS - 3:
                    later.power(pool, 0)

            pipeline(pool, prologue, sequence)

        @block.vector
        def _(dve):
            dve.wait_ge(constants.ready, constants.steps)

            def statistics(m, p):
                n = at(m, p)
                dve.bn_stats(stats[:], x_res[:, n, :]).then_inc(v_ln, 1)
                wait_before(dve, idle[:, 0:1], [(v_ln, 2 * n + 1)])
                dve.bn_aggr(mean_var[:], stats[:]).then_inc(v_ln, 1)
                dve.wait_ge(v_ln, 2 * n + 2)
                dve.tensor_scalar(var_eps[:], mean_var[:, 1:2], EPS, None, ALU.add).then_inc(v_var, 1)

            def normalize(m, p):
                n = at(m, p)
                dve.wait_ge(p_rstd, n + 1)
                if has(m, p, -2):
                    dve.wait_ge(pe_nt, n - 1)
                dve.tensor_scalar(normed[p][:], x_res[:, n, :], mean_var[:, 0:1], rstd[:, 0:1], ALU.subtract,
                                  ALU.mult).then_inc(v_norm, 1)

            def key_low(m, p):
                for k in range(KD):
                    dve.wait_ge(act_khi, KD * at(m, p) + k + 1)
                    for half in HALVES:
                        other = HALVES[half.start == 0]
                        g = 2 * k + (half.start > 0)
                        last = dve.tensor_tensor(keys[p][other, g, :], psum[half, KV + k, 0:CP],
                                                 keys[p][half, g, :].bitcast(F32), ALU.subtract)
                    last.then_inc(v_klo, 1)

            def queries_low(m, p):
                n = at(m, p)
                dve.wait_ge(act_qhi, n + 1)
                for half in HALVES:
                    g = int(half.start > 0)
                    for dst in HALVES:
                        last = dve.scalar_tensor_tensor(q_lo[dst, :, g, :], q_psum(half), 0.25,
                                                        q_hi[half, :, g, :].bitcast(F32), ALU.mult, ALU.subtract)
                last.then_inc(v_q, 1)

            def maxima(m, p, heads):
                n = at(m, p)
                for h in heads:
                    waits = [(pe_max, NH * n + h + 1)]
                    if h > 1 or has(m, p, -1):
                        waits.append((v_max, NH * n + h - 1))
                    if h == 0 and has(m, p, -1):
                        waits.append((pe_maxt, n))
                    wait_before(dve, idle[:, 1 + h:2 + h], waits)
                    dve.tensor_tensor_reduce(out=scored[h % 2][:], in0=psum[0:L, KV + (h + 1) % 2, 0:CP], in1=bias_row[:],
                                             scale=1.0, scalar=-3e38, op0=ALU.add, op1=ALU.max,
                                             accum_out=row_max[:, h:h + 1]).then_inc(v_max, 1)

            def place_shift(m, p):
                n = at(m, p)
                dve.wait_ge(pe_maxt, n + 1)
                if has(m, p, -2):
                    dve.wait_ge(pe_score, STEPS * (n - 1))
                dve.tensor_tensor(shift[p][0:NH, :].rearrange("h (j l) -> h j l", j=HG),
                                  bc_mid(max_t, HG), bc_last(place[:], L), ALU.mult
                                  ).then_inc(v_shift, 1)

            def normalize_o(m, p):
                n = at(m, p)
                src = psum[0:L, MISC, :].rearrange("l (h w) -> l h w", h=NH)
                dve.wait_ge(pe_ot, n + 1)
                dve.reciprocal(rden[:], src[:, :, DK]).then_inc(v_rden, 1)
                dve.wait_ge(v_rden, 2 * n + 1)
                dve.tensor_scalar(rden[:], rden[:], keep_row[:, 0:1], None, ALU.mult).then_inc(v_rden, 1)
                dve.wait_ge(v_rden, 2 * n + 2)
                dve.tensor_tensor(o_n[:], src[:, :, 0:DK], bc_last(rden[:], DK), ALU.mult).then_inc(v_on, 1)

            def residual(m, p):
                n = at(m, p)
                dve.wait_ge(pe_wo, n + 1)
                if has(m, p, -2):
                    dve.wait_ge(x2_out[p], 16 * m)
                dve.tensor_tensor(x2[p][:], psum[0:L, MISC, 0:D], x_res[:, n, :], ALU.add).then_inc(v_x2, 1)

            def prologue():
                statistics(0, 0)
                normalize(0, 0)
                statistics(0, 1)
                key_low(0, 0)
                queries_low(0, 0)
                normalize(0, 1)
                maxima(0, 0, range(NH))
                place_shift(0, 0)

            def sequence(m, p):
                nxt = after(m, p, 1) if has(m, p, 1) else None
                prv = after(m, p, -1) if has(m, p, -1) else None
                aft = after(m, p, 2) if has(m, p, 2) else None
                if nxt:
                    key_low(*nxt)
                if aft:
                    statistics(*aft)
                if nxt:
                    queries_low(*nxt)
                if aft:
                    normalize(*aft)
                if prv:
                    normalize_o(*prv)
                if nxt:
                    maxima(*nxt, range(NH))
                    place_shift(*nxt)
                if prv:
                    residual(*prv)
                if type(m) is int and 2 * m + p == SEQS - 3:
                    later.statistics(dve, 0, later.y_first)
                if type(m) is int and 2 * m + p == SEQS - 2:
                    later.normalize(dve, 0, later.y_first)

            pipeline(dve, prologue, sequence)
            last = (SEQS // 2 - 1, 1)
            normalize_o(*last)
            residual(*last)


TOKENS = SEQS * L
TILES = 5
BLOCK = TILES * P
BLOCKS = TOKENS // BLOCK
HALF = BLOCK // 2
EXPERTS, HIDDEN = 8, 512
KH = HIDDEN // P


class MoeStart:

    def __init__(self, nc, ctx, x_in, t):
        def sb(name, shape, dt=F32):
            return ctx.enter_context(nc.sbuf_tensor(name, shape, dt))

        def sem(name):
            return ctx.enter_context(nc.semaphore(name))

        self.t = t
        self.x_view = x_in.rearrange("(g j p) d -> g p j d", j=TILES, p=P)
        self.y_first = sb("y_first", [P, TILES, D])
        self.normed = sb("normed_f", [P, TILES, D])
        self.w1_raw = sb("w1_raw", [P, KD, HIDDEN])
        self.wg = sb("wg", [P, KD, EXPERTS])
        self.ident = sb("ident_f", [P, P])
        self.iota = sb("iota", [P, EXPERTS])
        self.neg_half = sb("neg_half_f", [P, TILES])
        self.stats = sb("stats_f", [P, TILES, 6])
        self.mean_var = sb("mean_var_f", [P, TILES, 2])
        self.var_eps = sb("var_eps_f", [P, TILES])
        self.rstd = sb("rstd_f", [P, TILES])
        self.idle = sb("idle_f", [P, 3])

        self.w_loaded = sem("f_w_loaded")
        self.x_loaded = sem("f_x_loaded")
        self.w1_in = sem("w1_in")
        self.prep = sem("f_prep")
        self.v_ln = sem("f_v_ln")
        self.v_var = sem("f_v_var")
        self.p_rstd = sem("f_p_rstd")
        self.v_norm = sem("f_v_norm")

    def load(self, sp):
        sp.dma_start(self.y_first[:], self.x_view[0]).then_inc(self.x_loaded, 16)
        for dst, src in ((self.wg[:], self.t["wg"].rearrange("(k p) e -> p k e", p=P)),
                         (self.ident[:], self.t["ident"]), (self.iota[:], self.t["iota"])):
            sp.dma_start(dst, src).then_inc(self.w_loaded, 16)
        self.load_w1(sp, 0)

    def load_w1(self, sp, e):
        sp.dma_start(self.w1_raw[:], self.t["w1"][e].rearrange("(k p) n -> p k n", p=P)).then_inc(self.w1_in, 16)

    def statistics(self, dve, g, rows):
        if type(g) is int and g == 0:
            dve.memset(self.neg_half[:], -0.5).then_inc(self.prep, 1)
        dve.wait_ge(self.x_loaded, 16 * (g + 1))
        for j in range(TILES):
            last = dve.bn_stats(self.stats[:, j, :], rows[:, j, :])
        last.then_inc(self.v_ln, 1)
        wait_before(dve, self.idle[:, 0:1], [(self.v_ln, 2 * g + 1)])
        for j in range(TILES):
            last = dve.bn_aggr(self.mean_var[:, j, :], self.stats[:, j, :])
        last.then_inc(self.v_ln, 1)
        dve.wait_ge(self.v_ln, 2 * g + 2)
        dve.tensor_scalar(self.var_eps[:], self.mean_var[:, :, 1], EPS, None, ALU.add).then_inc(self.v_var, 1)

    def power(self, pool, g):
        if type(g) is int and g == 0:
            pool.wait_ge(self.prep, 1)
        pool.wait_ge(self.v_var, g + 1)
        pool.tensor_tensor(self.rstd[:], self.var_eps[:], self.neg_half[:], ALU.pow).then_inc(self.p_rstd, 1)

    def normalize(self, dve, g, rows):
        dve.wait_ge(self.p_rstd, g + 1)
        for j in range(TILES):
            last = dve.tensor_scalar(self.normed[:, j, :], rows[:, j, :], self.mean_var[:, j, 0:1],
                                     self.rstd[:, j:j + 1], ALU.subtract, ALU.mult)
        last.then_inc(self.v_norm, 1)


def moe_block(nc, start, out, t):
    with ExitStack() as ctx:
        def sb(name, shape, dt=F32):
            return ctx.enter_context(nc.sbuf_tensor(name, shape, dt))

        def pair(name, shape, dt=F32):
            return [sb(f"{name}{i}", shape, dt) for i in range(2)]

        def sem(name):
            return ctx.enter_context(nc.semaphore(name))

        w1_hi = sb("w1_hi", [P, EXPERTS, KD, HIDDEN], F32R)
        w1_lo = sb("w1_lo", [P, EXPERTS, KD, HIDDEN], F32R)
        w2_hi = sb("w2_hi", [P, EXPERTS, KH, D], F32R)
        w2_lo = sb("w2_lo", [P, EXPERTS, KH, D], F32R)
        w2_raw = sb("w2_raw", [P, KH, D])

        wg, ident, iota, normed, idle = start.wg, start.ident, start.iota, start.normed, start.idle
        w1_raw, w1_in = start.w1_raw, start.w1_in
        w_loaded, x_loaded, v_norm = start.w_loaded, start.x_loaded, start.v_norm
        y = sb("y", [P, BLOCKS - 1, TILES, D])
        combine = sb("combine", [P, BLOCKS, TILES, EXPERTS])
        n_t = sb("n_t", [P, KD, BLOCK])
        x_hi = sb("x_hi", [P, KD, BLOCK], F32R)
        x_lo = sb("x_lo", [P, KD, BLOCK], F32R)
        gates = sb("gates", [P, TILES, EXPERTS])
        best = sb("best", [P, TILES, 8])
        best_at = sb("best_at", [P, TILES, 8], mybir.dt.uint32)
        best_f = sb("best_f", [P, TILES, 8])
        lead = sb("lead", [P, 2, TILES])
        share = sb("share", [P, 2, TILES])
        is_top = sb("is_top", [P, 2, TILES, EXPERTS])
        h = pair("h", [P, BLOCK])
        h_hi = pair("h_hi", [P, BLOCK], F32R)
        h_lo = pair("h_lo", [P, BLOCK], F32R)

        psum = ctx.enter_context(nc.psum_tensor("psum_f", [P, 8, 512], F32))
        HID, Y, MISC = 0, 4, 7

        w2_in = sem("w2_in")
        act_w1 = sem("act_w1")
        p_w1 = sem("p_w1")
        act_w2 = sem("act_w2")
        p_w2 = sem("p_w2")
        pe_nt = sem("f_pe_nt")
        act_nt = sem("f_act_nt")
        pe_gate = sem("pe_gate")
        v_gate = sem("v_gate")
        v_lead = sem("v_lead")
        act_share = sem("act_share")
        v_comb = sem("v_comb")
        v_xhi = sem("v_xhi")
        v_xlo = sem("v_xlo")
        pe_hid = sem("pe_hid")
        act_h = sem("act_h")
        v_hhi = sem("v_hhi")
        v_hlo = sem("v_hlo")
        pe_y = sem("f_pe_y")
        v_y = sem("v_y")
        stored = sem("stored")

        STEPS = EXPERTS * KH
        LAG = 2
        CHAIN = 7

        out_view = out.rearrange("(g j p) d -> g p j d", j=TILES, p=P)

        def rows(g):
            return start.y_first if type(g) is int and g == 0 else y[:, g - 1]

        def turned(g, j):
            return HID + j if type(g) is int and g == 0 else MISC

        def pipeline(eng, prepare, main):
            for piece in range(TRANSPOSE, SPLIT + 1):
                if piece != ROUTE:
                    prepare(0, piece)
            main(0, lambda piece: prepare(1, piece))
            with eng.Fori(1, BLOCKS - 1) as g:
                main(g, lambda piece: prepare(g + 1, piece))
            main(BLOCKS - 1, lambda piece: None)

        STATISTICS, NORMALIZE, TRANSPOSE = 0, 1, 2
        ROUTE, SPLIT = TRANSPOSE + TILES, TRANSPOSE + TILES + 1
        AT = {4: STATISTICS, 8: NORMALIZE, 12 + TILES + 2: ROUTE, **{12 + j: TRANSPOSE + j for j in range(TILES)}}

        block = ctx.enter_context(nc.Block())

        @block.sync
        def _(sp):
            def load_x(g):
                sp.dma_start(rows(g), start.x_view[g]).then_inc(x_loaded, 16)

            for e in range(EXPERTS):
                if e:
                    sp.wait_ge(p_w1, e)
                    start.load_w1(sp, e)
                if e:
                    sp.wait_ge(p_w2, e)
                sp.dma_start(w2_raw[:], t["w2"][e].rearrange("(k p) n -> p k n", p=P)).then_inc(w2_in, 16)
                if 0 < e < BLOCKS:
                    sp.wait_ge(x_loaded, 16 * e)
                    load_x(e)

            def store(g):
                sp.wait_ge(v_y, (g + 1) * EXPERTS * TILES)
                sp.dma_start(out_view[g], rows(g)[:]).then_inc(stored, 16)

            store(0)
            with sp.Fori(1, BLOCKS) as g:
                store(g)
            sp.wait_ge(stored, 16 * BLOCKS)

        @block.tensor
        def _(pe):
            pe.wait_ge(w_loaded, 16 * 3)

            def prepare(g, piece):
                if TRANSPOSE <= piece < ROUTE:
                    j = piece - TRANSPOSE
                    n = g * TILES + j
                    pe.wait_ge(v_norm, g + 1)
                    if j and not (type(g) is int and g == 0):
                        pe.wait_ge(act_nt, n)
                    elif not (type(g) is int and g == 0):
                        pe.wait_ge(v_gate, g)
                    for k in range(KD):
                        last = pe.transpose(psum[:, turned(g, j), k * P:(k + 1) * P],
                                            normed[:, j, k * P:(k + 1) * P], ident[:])
                    last.then_inc(pe_nt, 1)
                if piece == ROUTE:
                    pe.wait_ge(act_nt, (g + 1) * TILES)
                    for j in range(TILES):
                        for k in range(KD):
                            last = pe.matmul(psum[:, MISC, j * EXPERTS:(j + 1) * EXPERTS],
                                             n_t[:, k, j * P:(j + 1) * P], wg[:, k, :], start=k == 0,
                                             stop=k == KD - 1)
                    last.then_inc(pe_gate, 1)

            def hidden(g, s):
                e, m = s // KH, s % KH
                n = g * STEPS + s
                if s == 0:
                    pe.wait_ge(v_xlo, g + 1)
                if m == 0 and type(g) is int and g == 0:
                    pe.wait_ge(p_w1, e + 1)
                if not (type(g) is int and g == 0 and s < 2):
                    pe.wait_ge(act_h, n - 1)
                cols = slice(m * P, (m + 1) * P)
                for d in range(KD):
                    for a, b in ((w1_hi, x_hi), (w1_lo, x_hi), (w1_hi, x_lo)):
                        for half in range(2):
                            last = pe.matmul(psum[:, HID + 2 * (s % 2) + half, 0:HALF], a[:, e, d, cols],
                                             b[:, d, half * HALF:(half + 1) * HALF], start=d == 0 and a is w1_hi
                                             and b is x_hi, stop=d == KD - 1 and b is x_lo)
                last.then_inc(pe_hid, 1)

            def outputs(g, s):
                e, m = s // KH, s % KH
                n = g * STEPS + s
                if m == 0 and type(g) is int and g == 0:
                    pe.wait_ge(p_w2, e + 1)
                pe.wait_ge(v_hlo, n + 1)
                for j in range(TILES):
                    if m == 0 and j % 2 == 0 and not (type(g) is int and g == 0 and e == 0):
                        pe.wait_ge(v_y, (g * EXPERTS + e - 1) * TILES + min(j + 2, TILES))
                    rows = slice(j * P, (j + 1) * P)
                    dst = psum[:, Y + j // 2, (j % 2) * D:(j % 2 + 1) * D]
                    pe.matmul(dst, h_hi[s % 2][:, rows], w2_hi[:, e, m, :], start=m == 0 and j % 2 == 0, stop=False,
                              skip_group_check=True)
                    pe.matmul(dst, h_lo[s % 2][:, rows], w2_hi[:, e, m, :], start=False, stop=False,
                              skip_group_check=True)
                    last = pe.matmul(dst, h_hi[s % 2][:, rows], w2_lo[:, e, m, :], start=False, stop=m == KH - 1,
                                     skip_group_check=True)
                last.then_inc(pe_y, 1)

            def main(g, more):
                for s in range(STEPS):
                    hidden(g, s)
                    if s == LAG and type(g) is int and g == 0:
                        prepare(0, ROUTE)
                    if s >= LAG:
                        outputs(g, s - LAG)
                    if s in AT:
                        more(AT[s])
                for s in range(STEPS - LAG, STEPS):
                    outputs(g, s)

            pipeline(pe, prepare, main)

        @block.scalar
        def _(act):
            def w1_high(e):
                act.wait_ge(w1_in, 16 * (e + 1))
                act.copy(w1_hi[:, e], w1_raw[:]).then_inc(act_w1, 1)

            def w2_high(e):
                act.wait_ge(w2_in, 16 * (e + 1))
                act.copy(w2_hi[:, e], w2_raw[:]).then_inc(act_w2, 1)

            w1_high(0)

            def prepare(g, piece):
                if TRANSPOSE <= piece < ROUTE:
                    j = piece - TRANSPOSE
                    act.wait_ge(pe_nt, g * TILES + j + 1)
                    act.copy(n_t[:, :, j * P:(j + 1) * P], psum[:, turned(g, j), 0:KD * P].rearrange(
                        "p (k l) -> p k l", k=KD)).then_inc(act_nt, 1)
                if piece == ROUTE:
                    act.wait_ge(v_lead, g + 1)
                    act.activation(share[:], lead[:], ACT.Tanh, scale=0.5).then_inc(act_share, 1)

            def main(g, more):
                if type(g) is int and g == 0:
                    w2_high(0)
                for s in range(STEPS):
                    n = g * STEPS + s
                    act.wait_ge(pe_hid, n + 1)
                    if not (type(g) is int and g == 0 and s < 2):
                        act.wait_ge(v_hlo, n - 1)
                    act.activation(h[s % 2][:].rearrange("p (a b) -> p a b", a=2),
                                   psum[:, HID + 2 * (s % 2):HID + 2 * (s % 2) + 2, 0:HALF], ACT.Silu
                                   ).then_inc(act_h, 1)
                    if type(g) is int and g == 0:
                        if s % KH == 0 and s // KH + 1 < EXPERTS:
                            w1_high(s // KH + 1)
                            w2_high(s // KH + 1)
                        if s == LAG:
                            prepare(0, ROUTE)
                    if s in AT:
                        more(AT[s])

            pipeline(act, prepare, main)

        @block.gpsimd
        def _(pool):
            def prepare(g, piece):
                if piece == STATISTICS:
                    start.power(pool, g)

            def weights_low(e):
                pool.wait_ge(act_w1, e + 1)
                pool.tensor_tensor(w1_lo[:, e], w1_raw[:], w1_hi[:, e].bitcast(F32), ALU.subtract).then_inc(p_w1, 1)
                pool.wait_ge(act_w2, e + 1)
                pool.tensor_tensor(w2_lo[:, e], w2_raw[:], w2_hi[:, e].bitcast(F32), ALU.subtract).then_inc(p_w2, 1)

            def main(g, more):
                if type(g) is int and g == 0:
                    for e in range(2):
                        weights_low(e)
                more(STATISTICS)
                if type(g) is int and g == 0:
                    for e in range(2, EXPERTS):
                        weights_low(e)

            pipeline(pool, prepare, main)

        @block.vector
        def _(dve):
            dve.wait_ge(w_loaded, 16 * 3)

            def routing(g):
                step = [0]

                def then(ins):
                    step[0] += 1
                    if step[0] == 1:
                        ins.then_inc(v_gate, 1)
                        waits = [(v_gate, g + 1)]
                    else:
                        ins.then_inc(v_comb, 1)
                        waits = [(v_comb, g * CHAIN + step[0] - 1)]
                    if step[0] < 3:
                        wait_before(dve, idle[:, step[0]:step[0] + 1], waits)
                    else:
                        dve.wait_ge(*waits[0])

                tiles = slice(0, TILES)
                dve.wait_ge(pe_gate, g + 1)
                then(dve.tensor_copy(gates[:], psum[:, MISC, 0:TILES * EXPERTS].rearrange("p (j e) -> p j e", j=TILES)))
                for j in range(TILES):
                    last = dve.max(best[:, j, :], gates[:, j, :])
                then(last)
                for j in range(TILES):
                    last = dve.max_index(best_at[:, j, :], best[:, j, :], gates[:, j, :])
                then(last)
                then(dve.tensor_copy(best_f[:], best_at[:]))
                dve.tensor_tensor(lead[:, 0, tiles], best[:, :, 0], best[:, :, 1], ALU.subtract)
                dve.tensor_tensor(lead[:, 1, tiles], best[:, :, 1], best[:, :, 0], ALU.subtract).then_inc(v_lead, 1)
                dve.tensor_tensor(is_top[:, 0], bc_mid(iota[:], TILES), bc_last(best_f[:, :, 0], EXPERTS), ALU.is_equal)
                then(dve.tensor_tensor(is_top[:, 1], bc_mid(iota[:], TILES), bc_last(best_f[:, :, 1], EXPERTS),
                                       ALU.is_equal))
                dve.wait_ge(act_share, g + 1)
                then(dve.tensor_scalar(lead[:], share[:], 0.5, 0.5, ALU.mult, ALU.add))
                dve.tensor_tensor(is_top[:, 0], is_top[:, 0], bc_last(lead[:, 0, :], EXPERTS), ALU.mult)
                then(dve.tensor_tensor(is_top[:, 1], is_top[:, 1], bc_last(lead[:, 1, :], EXPERTS), ALU.mult))
                then(dve.tensor_tensor(combine[:, g], is_top[:, 0], is_top[:, 1], ALU.add))
                assert step[0] == CHAIN + 1

            def prepare(g, piece):
                if piece == STATISTICS:
                    start.statistics(dve, g, rows(g))
                if piece == NORMALIZE:
                    start.normalize(dve, g, rows(g))
                if piece == ROUTE:
                    routing(g)
                if piece == SPLIT:
                    dve.wait_ge(act_nt, (g + 1) * TILES)
                    if not (type(g) is int and g == 0):
                        dve.wait_ge(pe_hid, g * STEPS)
                    dve.tensor_copy(x_hi[:], n_t[:]).then_inc(v_xhi, 1)
                    dve.wait_ge(v_xhi, g + 1)
                    dve.tensor_tensor(x_lo[:], n_t[:], x_hi[:].bitcast(F32), ALU.subtract).then_inc(v_xlo, 1)

            def add_outputs(g, e):
                dve.wait_ge(pe_y, g * STEPS + (e + 1) * KH)
                for j in range(TILES):
                    dve.scalar_tensor_tensor(rows(g)[:, j, :], psum[:, Y + j // 2, (j % 2) * D:(j % 2 + 1) * D],
                                             combine[:, g, j, e:e + 1], rows(g)[:, j, :], ALU.mult, ALU.add).then_inc(v_y, 1)

            def main(g, more):
                first = type(g) is int and g == 0
                for s in range(STEPS):
                    n = g * STEPS + s
                    if first and s == LAG:
                        prepare(0, ROUTE)
                    if s % KH == 1 and s > KH:
                        add_outputs(g, s // KH - 1)
                    dve.wait_ge(act_h, n + 1)
                    if not (first and s < 2):
                        dve.wait_ge(pe_y, n - 1)
                    dve.tensor_copy(h_hi[s % 2][:], h[s % 2][:]).then_inc(v_hhi, 1)
                    dve.wait_ge(v_hhi, n + 1)
                    dve.tensor_tensor(h_lo[s % 2][:], h[s % 2][:], h_hi[s % 2][:].bitcast(F32), ALU.subtract
                                      ).then_inc(v_hlo, 1)
                    if s in AT:
                        more(AT[s])
                more(SPLIT)
                add_outputs(g, EXPERTS - 1)

            pipeline(dve, prepare, main)


def build_decoder(nc, t, out):
    x2 = nc.dram_tensor("x2_scratch", (SEQS, L, D), F32).ap()
    with ExitStack() as outer:
        moe_start = MoeStart(nc, outer, x2.rearrange("s l d -> (s l) d"), t)
        with ExitStack() as ctx:
            x_res = ctx.enter_context(nc.sbuf_tensor("x_res", [L, SEQS, D], F32))
            cross_constants = CrossConstants(nc, ctx, t)
            mamba_block(nc, x_res, t, cross_constants)
            cross_block(nc, x_res, x2, cross_constants, moe_start)
        moe_block(nc, moe_start, out.rearrange("s l d -> (s l) d"), t)


def constants():
    eye = np.eye(P, dtype=np.float32)
    square = np.ones((L, L), np.float32)
    row, head = np.arange(P)[:, None], np.arange(NH)[:, None]
    group = np.arange(HG)[None]
    return {
        "ident": eye,
        "ones": np.ones((P, 1), np.float32),
        "upto": np.triu(square),
        "after": np.tril(square, -1),
        "block4": (row % (HG * DK) // DK == group).astype(np.float32),
        "pick": (head // HG == group).astype(np.float32),
        "place": -(head % HG == group).astype(np.float32),
        "shift": np.concatenate([np.zeros((NH, HG * L), np.float32), np.tile(eye[:L, :L], (1, HG))]),
        "iota": np.tile(np.arange(EXPERTS, dtype=np.float32), (P, 1)),
    }


def kernel(**inputs):
    import concourse.bacc as bacc
    from concourse.bass_utils import run_bass_kernel_spmd

    a = {name: np.asarray(value) for name, value in inputs.items()}

    def columns(v):
        return v.reshape(-1, P).T

    def heads(w):
        return w.transpose(1, 0, 2).reshape(D, NH * DK)

    laid = {
        "x": a["x"],
        "w_in": a["L0_attn_in_proj_w"].T,
        "w_out": a["L0_attn_out_proj_w"].T,
        "ln_w": columns(a["L0_attn_ln_w"]),
        "ln_b": columns(a["L0_attn_ln_b"]),
        "conv_w": a["L0_attn_conv_w"],
        "conv_b": columns(a["L0_attn_conv_b"]),
        "gamma": columns(a["L0_attn_gamma"]),
        "a_log": a["L0_attn_A_log"],
        "dt_bias": a["L0_attn_dt_bias"],
        "d_even": a["L0_attn_D"][0::2],
        "d_odd": a["L0_attn_D"][1::2],
        "ctx_t": a["ctx_1024"].transpose(0, 2, 1),
        "mask": a["mask_SxS2_ik0"],
        "wq": heads(a["L0_xattn_Wq"]),
        "wk": heads(a["L0_xattn_Wk"]),
        "wv": heads(a["L0_xattn_Wv"]),
        "wo": a["L0_xattn_Wo"].T,
        "wg": a["L0_ffn_Wg"],
        "w1": a["L0_ffn_W1"],
        "w2": a["L0_ffn_W2"],
        **constants(),
    }
    nc = bacc.Bacc("TRN2", target_bir_lowering=False, num_devices=1)
    arrays, t = {}, {}
    for name, value in laid.items():
        value = np.ascontiguousarray(value)
        arrays[f"in_{name}"] = value
        t[name] = nc.dram_tensor(f"in_{name}", value.shape, mybir.dt.from_np(value.dtype), kind="ExternalInput").ap()
    out = nc.dram_tensor("out", (SEQS, L, D), F32, kind="ExternalOutput").ap()
    build_decoder(nc, t, out)
    r = run_bass_kernel_spmd(nc, [arrays], core_ids=[0])
    return r.results[0]["out"]
```
